# Optimizing a Trainium2 kernel written in Bass

```python
import numpy as np
import jax
import jax.numpy as jnp

def _softmax(x, axis=-1):
    return jax.nn.softmax(x, axis=axis)

def _gelu(x):
    return jax.nn.gelu(x, approximate=True)

def _silu(x):
    return jax.nn.silu(x)

def _sigmoid(x):
    return jax.nn.sigmoid(x)

def _layernorm(x, axis=-1, eps=1e-05):
    m = jnp.mean(x, axis=axis, keepdims=True)
    v = jnp.var(x, axis=axis, keepdims=True)
    return (x - m) / jnp.sqrt(v + eps)

def _scatter_add(tgt, idx, src, axis=0):
    return tgt.at[idx].add(src)

def _segment_sum(src, seg, n):
    return jax.ops.segment_sum(src, seg, n)
kernel_name = 'mk_seq_postln_d2_jaxref_r8_f47c53'

def setup_inputs(seed: int=0):
    np.random.seed(seed)
    _w = jnp.asarray

    def _L0_attn_setup():
        import jax, jax.numpy as jnp
        import numpy as np
        D_MODEL = 128
        N_HEADS = 16
        LOCAL_W = 128
        GLOBAL_W = 128
        LN_EPS = 1e-05

        def _mha(x, W_in, b_in, W_out, b_out, mask):
            B, T, D = x.shape
            hd = D // N_HEADS
            qkv = x @ W_in.T + b_in
            q, k, v = jnp.split(qkv, 3, axis=-1)

            def heads(t):
                return t.reshape(B, T, N_HEADS, hd).transpose(0, 2, 1, 3)
            q, k, v = (heads(q), heads(k), heads(v))
            scale = 1.0 / jnp.sqrt(jnp.asarray(hd, x.dtype))
            scores = jnp.einsum('bhqd,bhkd->bhqk', q, k) * scale + mask
            a = jax.nn.softmax(scores, axis=-1)
            o = jnp.einsum('bhqk,bhkd->bhqd', a, v).transpose(0, 2, 1, 3).reshape(B, T, D)
            return o @ W_out.T + b_out

        def _sliding_window_attn(q, W_in, b_in, W_out, b_out, window):
            B, S, D = q.shape
            nw = (S + window - 1) // window
            pad = nw * window - S
            if pad > 0:
                q = jnp.pad(q, ((0, 0), (0, pad), (0, 0)))
            qw = q.reshape(B * nw, window, D)
            mask = jnp.triu(jnp.ones((window, window), dtype=q.dtype), k=1)
            out = _mha(qw, W_in, b_in, W_out, b_out, mask)
            return out.reshape(B, nw * window, D)[:, :S, :]
        key = jax.random.key(seed)
        ks = jax.random.split(key, 12)
        D = D_MODEL
        s = 1.0 / np.sqrt(D)
        pl, _ = jnp.linalg.qr(jax.random.normal(ks[0], (D, D), jnp.float32))
        pg, _ = jnp.linalg.qr(jax.random.normal(ks[1], (D, D), jnp.float32))
        return {'x': jax.random.normal(ks[2], (2, 512, D), jnp.float32), 'proj_local': pl, 'proj_global': pg, 'Wl_in': jax.random.uniform(ks[3], (3 * D, D), jnp.float32, -s, s), 'bl_in': jnp.zeros((3 * D,), jnp.float32), 'Wl_out': jax.random.uniform(ks[4], (D, D), jnp.float32, -s, s), 'bl_out': jnp.zeros((D,), jnp.float32), 'Wg_in': jax.random.uniform(ks[5], (3 * D, D), jnp.float32, -s, s), 'bg_in': jnp.zeros((3 * D,), jnp.float32), 'Wg_out': jax.random.uniform(ks[6], (D, D), jnp.float32, -s, s), 'bg_out': jnp.zeros((D,), jnp.float32), 'fusion_w': jnp.ones((2,), jnp.float32), 'ln_gamma': jnp.ones((D,), jnp.float32), 'ln_beta': jnp.zeros((D,), jnp.float32)}
    _L0_attn_in = _L0_attn_setup()

    def _L0_ffn_setup():
        import jax, jax.numpy as jnp
        import numpy as np
        DIM = 128

        def _reference_tuple_inner(x, W_r, W_k, W_v, mu_r, mu_k):
            B, T, C = x.shape
            x_prev = jnp.concatenate([jnp.zeros((B, 1, C), x.dtype), x[:, :-1, :]], axis=1)
            xr = mu_r * x + (1.0 - mu_r) * x_prev
            xk = mu_k * x + (1.0 - mu_k) * x_prev
            r = jax.nn.sigmoid(jnp.einsum('btc,dc->btd', xr, W_r))
            k = jnp.einsum('btc,dc->btd', xk, W_k)
            k_act = jnp.square(jax.nn.relu(k))
            out = r * jnp.einsum('btc,dc->btd', k_act, W_v)
            new_state = x[:, -1, :]
            return (out, new_state)
        key = jax.random.key(seed)
        ks = jax.random.split(key, 6)
        B, T, C = (8, 256, DIM)
        x = jax.random.normal(ks[0], (B, T, C), dtype=jnp.float32)
        s = 1.0 / np.sqrt(C)
        W_r = jax.random.uniform(ks[1], (C, C), jnp.float32, -s, s)
        W_k = jax.random.uniform(ks[2], (C, C), jnp.float32, -s, s)
        W_v = jax.random.uniform(ks[3], (C, C), jnp.float32, -s, s)
        mu_r = jax.random.uniform(ks[4], (C,), jnp.float32)
        mu_k = jax.random.uniform(ks[5], (C,), jnp.float32)
        return {'x': x, 'W_r': W_r, 'W_k': W_k, 'W_v': W_v, 'mu_r': mu_r, 'mu_k': mu_k}
    _L0_ffn_in = _L0_ffn_setup()

    def _L1_attn_setup():
        import jax, jax.numpy as jnp
        import numpy as np
        EPS = 1e-06
        NUM_HEADS = 16

        def _phi(x):
            return jax.nn.elu(x) + 1.0
        key = jax.random.key(seed)
        ks = jax.random.split(key, 5)
        B, S, D = (2, 256, 128)
        scale = 1.0 / np.sqrt(D)
        return {'x': jax.random.normal(ks[0], (B, S, D), dtype=jnp.float32), 'Wq': jax.random.normal(ks[1], (D, D), dtype=jnp.float32) * scale, 'bq': jnp.zeros((D,), dtype=jnp.float32), 'Wk': jax.random.normal(ks[2], (D, D), dtype=jnp.float32) * scale, 'bk': jnp.zeros((D,), dtype=jnp.float32), 'Wv': jax.random.normal(ks[3], (D, D), dtype=jnp.float32) * scale, 'bv': jnp.zeros((D,), dtype=jnp.float32), 'Wo': jax.random.normal(ks[4], (D, D), dtype=jnp.float32) * scale, 'bo': jnp.zeros((D,), dtype=jnp.float32)}
    _L1_attn_in = _L1_attn_setup()

    def _L1_ffn_setup():
        import jax, jax.numpy as jnp
        import numpy as np
        D_IN, D_HID = (128, 512)

        def _ternary(key, shape):
            return jax.random.randint(key, shape, -1, 2).astype(jnp.float32)

        def _tlin(x, w, s):
            return jnp.einsum('bsi,oi->bso', x, w) * s
        key = jax.random.key(seed)
        ks = jax.random.split(key, 12)
        inv = lambda fan: 1.0 / np.sqrt(fan).astype(np.float32)
        return {'x': jax.random.normal(ks[0], (4, 256, D_IN), dtype=jnp.float32), 'w1_w': _ternary(ks[1], (D_HID, D_IN)), 'w1_s': jax.random.uniform(ks[2], (D_HID,), dtype=jnp.float32) * inv(D_IN), 'w2_w': _ternary(ks[3], (D_HID, D_IN)), 'w2_s': jax.random.uniform(ks[4], (D_HID,), dtype=jnp.float32) * inv(D_IN), 'h1_w': _ternary(ks[5], (D_HID, D_HID)), 'h1_s': jax.random.uniform(ks[6], (D_HID,), dtype=jnp.float32) * inv(D_HID), 'h2_w': _ternary(ks[7], (D_HID, D_HID)), 'h2_s': jax.random.uniform(ks[8], (D_HID,), dtype=jnp.float32) * inv(D_HID), 'w3_w': _ternary(ks[9], (D_IN, D_HID)), 'w3_s': jax.random.uniform(ks[10], (D_IN,), dtype=jnp.float32) * inv(D_HID)}
    _L1_ffn_in = _L1_ffn_setup()
    _d = {'L0_attn_x': _L0_attn_in['x'], 'L0_attn_proj_local': _L0_attn_in['proj_local'], 'L0_attn_proj_global': _L0_attn_in['proj_global'], 'L0_attn_Wl_in': _L0_attn_in['Wl_in'], 'L0_attn_bl_in': _L0_attn_in['bl_in'], 'L0_attn_Wl_out': _L0_attn_in['Wl_out'], 'L0_attn_bl_out': _L0_attn_in['bl_out'], 'L0_attn_Wg_in': _L0_attn_in['Wg_in'], 'L0_attn_bg_in': _L0_attn_in['bg_in'], 'L0_attn_Wg_out': _L0_attn_in['Wg_out'], 'L0_attn_bg_out': _L0_attn_in['bg_out'], 'L0_attn_fusion_w': _L0_attn_in['fusion_w'], 'L0_attn_ln_gamma': _L0_attn_in['ln_gamma'], 'L0_attn_ln_beta': _L0_attn_in['ln_beta'], 'L0_ffn_W_r': _L0_ffn_in['W_r'], 'L0_ffn_W_k': _L0_ffn_in['W_k'], 'L0_ffn_W_v': _L0_ffn_in['W_v'], 'L0_ffn_mu_r': _L0_ffn_in['mu_r'], 'L0_ffn_mu_k': _L0_ffn_in['mu_k'], 'L1_attn_Wq': _L1_attn_in['Wq'], 'L1_attn_bq': _L1_attn_in['bq'], 'L1_attn_Wk': _L1_attn_in['Wk'], 'L1_attn_bk': _L1_attn_in['bk'], 'L1_attn_Wv': _L1_attn_in['Wv'], 'L1_attn_bv': _L1_attn_in['bv'], 'L1_attn_Wo': _L1_attn_in['Wo'], 'L1_attn_bo': _L1_attn_in['bo'], 'L1_ffn_w1_w': _L1_ffn_in['w1_w'], 'L1_ffn_w1_s': _L1_ffn_in['w1_s'], 'L1_ffn_w2_w': _L1_ffn_in['w2_w'], 'L1_ffn_w2_s': _L1_ffn_in['w2_s'], 'L1_ffn_h1_w': _L1_ffn_in['h1_w'], 'L1_ffn_h1_s': _L1_ffn_in['h1_s'], 'L1_ffn_h2_w': _L1_ffn_in['h2_w'], 'L1_ffn_h2_s': _L1_ffn_in['h2_s'], 'L1_ffn_w3_w': _L1_ffn_in['w3_w'], 'L1_ffn_w3_s': _L1_ffn_in['w3_s']}
    _x0 = _d['L0_attn_x']
    _d['L0_attn_x'] = jax.random.normal(jax.random.fold_in(jax.random.key(seed), 1), (8, 1024, 128), dtype=_x0.dtype)
    del _x0
    return _d

def reference(L0_attn_x, L0_attn_proj_local, L0_attn_proj_global, L0_attn_Wl_in, L0_attn_bl_in, L0_attn_Wl_out, L0_attn_bl_out, L0_attn_Wg_in, L0_attn_bg_in, L0_attn_Wg_out, L0_attn_bg_out, L0_attn_fusion_w, L0_attn_ln_gamma, L0_attn_ln_beta, L0_ffn_W_r, L0_ffn_W_k, L0_ffn_W_v, L0_ffn_mu_r, L0_ffn_mu_k, L1_attn_Wq, L1_attn_bq, L1_attn_Wk, L1_attn_bk, L1_attn_Wv, L1_attn_bv, L1_attn_Wo, L1_attn_bo, L1_ffn_w1_w, L1_ffn_w1_s, L1_ffn_w2_w, L1_ffn_w2_s, L1_ffn_h1_w, L1_ffn_h1_s, L1_ffn_h2_w, L1_ffn_h2_s, L1_ffn_w3_w, L1_ffn_w3_s):

    def _L0_attn_ref(x, proj_local, proj_global, Wl_in, bl_in, Wl_out, bl_out, Wg_in, bg_in, Wg_out, bg_out, fusion_w, ln_gamma, ln_beta):
        import jax, jax.numpy as jnp
        import numpy as np
        D_MODEL = 128
        N_HEADS = 16
        LOCAL_W = 128
        GLOBAL_W = 128
        LN_EPS = 1e-05

        def _mha(x, W_in, b_in, W_out, b_out, mask):
            B, T, D = x.shape
            hd = D // N_HEADS
            qkv = x @ W_in.T + b_in
            q, k, v = jnp.split(qkv, 3, axis=-1)

            def heads(t):
                return t.reshape(B, T, N_HEADS, hd).transpose(0, 2, 1, 3)
            q, k, v = (heads(q), heads(k), heads(v))
            scale = 1.0 / jnp.sqrt(jnp.asarray(hd, x.dtype))
            scores = jnp.einsum('bhqd,bhkd->bhqk', q, k) * scale + mask
            a = jax.nn.softmax(scores, axis=-1)
            o = jnp.einsum('bhqk,bhkd->bhqd', a, v).transpose(0, 2, 1, 3).reshape(B, T, D)
            return o @ W_out.T + b_out

        def _sliding_window_attn(q, W_in, b_in, W_out, b_out, window):
            B, S, D = q.shape
            nw = (S + window - 1) // window
            pad = nw * window - S
            if pad > 0:
                q = jnp.pad(q, ((0, 0), (0, pad), (0, 0)))
            qw = q.reshape(B * nw, window, D)
            mask = jnp.triu(jnp.ones((window, window), dtype=q.dtype), k=1)
            out = _mha(qw, W_in, b_in, W_out, b_out, mask)
            return out.reshape(B, nw * window, D)[:, :S, :]
        lqs = x @ proj_local
        gqs = x @ proj_global
        local_out = _sliding_window_attn(lqs, Wl_in, bl_in, Wl_out, bl_out, LOCAL_W)
        global_out = _sliding_window_attn(gqs, Wg_in, bg_in, Wg_out, bg_out, GLOBAL_W)
        w = jax.nn.softmax(fusion_w, axis=0)
        fused = w[0] * local_out + w[1] * global_out
        mu = jnp.mean(fused, axis=-1, keepdims=True)
        var = jnp.mean(jnp.square(fused - mu), axis=-1, keepdims=True)
        return (fused - mu) * jax.lax.rsqrt(var + LN_EPS) * ln_gamma + ln_beta

    def _L0_ffn_ref(x, W_r, W_k, W_v, mu_r, mu_k):
        import jax, jax.numpy as jnp
        import numpy as np
        DIM = 128

        def _reference_tuple_inner(x, W_r, W_k, W_v, mu_r, mu_k):
            B, T, C = x.shape
            x_prev = jnp.concatenate([jnp.zeros((B, 1, C), x.dtype), x[:, :-1, :]], axis=1)
            xr = mu_r * x + (1.0 - mu_r) * x_prev
            xk = mu_k * x + (1.0 - mu_k) * x_prev
            r = jax.nn.sigmoid(jnp.einsum('btc,dc->btd', xr, W_r))
            k = jnp.einsum('btc,dc->btd', xk, W_k)
            k_act = jnp.square(jax.nn.relu(k))
            out = r * jnp.einsum('btc,dc->btd', k_act, W_v)
            new_state = x[:, -1, :]
            return (out, new_state)
        return _reference_tuple_inner(x, W_r, W_k, W_v, mu_r, mu_k)[0]

    def _L1_attn_ref(x, Wq, bq, Wk, bk, Wv, bv, Wo, bo):
        import jax, jax.numpy as jnp
        import numpy as np
        EPS = 1e-06
        NUM_HEADS = 16

        def _phi(x):
            return jax.nn.elu(x) + 1.0
        B, S, D = x.shape
        H = NUM_HEADS
        hd = D // H
        q = (x @ Wq.T + bq).reshape(B, S, H, hd).transpose(0, 2, 1, 3)
        k = (x @ Wk.T + bk).reshape(B, S, H, hd).transpose(0, 2, 1, 3)
        v = (x @ Wv.T + bv).reshape(B, S, H, hd).transpose(0, 2, 1, 3)
        q = _phi(q)
        k = _phi(k)
        kv_cum = jnp.cumsum(k[..., :, None] * v[..., None, :], axis=2)
        k_cum = jnp.cumsum(k, axis=2)
        num = jnp.einsum('bhsd,bhsde->bhse', q, kv_cum)
        den = jnp.einsum('bhsd,bhsd->bhs', q, k_cum)
        out = num / (den[..., None] + EPS)
        out = out.transpose(0, 2, 1, 3).reshape(B, S, D)
        return out @ Wo.T + bo

    def _L1_ffn_ref(x, w1_w, w1_s, w2_w, w2_s, h1_w, h1_s, h2_w, h2_s, w3_w, w3_s):
        import jax, jax.numpy as jnp
        import numpy as np
        D_IN, D_HID = (128, 512)

        def _ternary(key, shape):
            return jax.random.randint(key, shape, -1, 2).astype(jnp.float32)

        def _tlin(x, w, s):
            return jnp.einsum('bsi,oi->bso', x, w) * s
        h = jax.nn.silu(_tlin(x, w1_w, w1_s)) * _tlin(x, w2_w, w2_s)
        h = jax.nn.gelu(_tlin(h, h1_w, h1_s), approximate=False)
        h = jax.nn.gelu(_tlin(h, h2_w, h2_s), approximate=False)
        return _tlin(h, w3_w, w3_s)
    x = L0_attn_x
    x = _layernorm(x + _L0_attn_ref(x, L0_attn_proj_local, L0_attn_proj_global, L0_attn_Wl_in, L0_attn_bl_in, L0_attn_Wl_out, L0_attn_bl_out, L0_attn_Wg_in, L0_attn_bg_in, L0_attn_Wg_out, L0_attn_bg_out, L0_attn_fusion_w, L0_attn_ln_gamma, L0_attn_ln_beta), axis=-1)
    x = _layernorm(x + _L0_ffn_ref(x, L0_ffn_W_r, L0_ffn_W_k, L0_ffn_W_v, L0_ffn_mu_r, L0_ffn_mu_k), axis=-1)
    x = _layernorm(x + _L1_attn_ref(x, L1_attn_Wq, L1_attn_bq, L1_attn_Wk, L1_attn_bk, L1_attn_Wv, L1_attn_bv, L1_attn_Wo, L1_attn_bo), axis=-1)
    x = _layernorm(x + _L1_ffn_ref(x, L1_ffn_w1_w, L1_ffn_w1_s, L1_ffn_w2_w, L1_ffn_w2_s, L1_ffn_h1_w, L1_ffn_h1_s, L1_ffn_h2_w, L1_ffn_h2_s, L1_ffn_w3_w, L1_ffn_w3_s), axis=-1)
    return x

_drawn_inputs = setup_inputs


def setup_inputs(seed=0):
    import zlib

    import numpy as np

    out = dict(_drawn_inputs(seed))
    spreads = {'L0_attn_bl_in': (0.0, 0.1),
     'L0_attn_bl_out': (0.0, 0.1),
     'L0_attn_bg_in': (0.0, 0.1),
     'L0_attn_bg_out': (0.0, 0.1),
     'L0_attn_fusion_w': (1.0, 0.6),
     'L0_attn_ln_gamma': (1.0, 0.2),
     'L0_attn_ln_beta': (0.0, 0.1),
     'L1_attn_bq': (0.0, 0.8),
     'L1_attn_bk': (0.0, 0.8),
     'L1_attn_bv': (0.0, 0.1),
     'L1_attn_bo': (0.0, 0.1)}
    factors = {'L0_ffn_W_r': 3.113,
     'L0_ffn_mu_r': 8.0,
     'L1_attn_Wq': 6.597,
     'L1_attn_Wk': 3.847,
     'L1_ffn_w1_w': 8.0,
     'L1_ffn_w1_s': 8.0,
     'L1_ffn_w2_w': 8.0,
     'L1_ffn_w2_s': 8.0,
     'L1_ffn_h1_w': 8.0,
     'L1_ffn_h1_s': 8.0,
     'L1_ffn_h2_w': 8.0,
     'L1_ffn_h2_s': 8.0,
     'L1_ffn_w3_w': 8.0,
     'L1_ffn_w3_s': 8.0}
    for name, (base, spread) in spreads.items():
        noise = np.random.default_rng([zlib.crc32(name.encode()), seed]).standard_normal(out[name].shape)
        drawn = base * np.exp(spread * noise) if base else spread * noise
        out[name] = jnp.asarray(drawn.astype(out[name].dtype))
    for name, factor in factors.items():
        out[name] = (out[name] * factor).astype(out[name].dtype)
    return out
```

```python
from contextlib import ExitStack

import numpy as np

import concourse.bass as bass
from concourse import mybir

F32 = mybir.dt.float32
BF16 = mybir.dt.bfloat16
ALU = mybir.AluOpType
ACT = mybir.ActivationFunctionType
AX = mybir.AxisListType

P = 128
BATCH, SEQ = 8, 1024
TILES = BATCH * SEQ // P
PER_BATCH = SEQ // P
HEADS, HD = 16, 8
J = 4
G = HEADS // J
HIDDEN = 512
HC = HIDDEN // P
GT = 4
GROUPS = TILES // GT
NE = HD + 1
EPS = 1e-5
EPS_LINEAR = 1e-6
SPLIT = [(0, 6), (6, 11), (11, 16)]

C_ID, C_UT, C_ONE, C_TRI = 0, P, 2 * P, 3 * P
C_MQ = C_TRI + P
C_MK = C_MQ + J
C_MM = C_MK + G
C_EG = C_MM + J
C_END = C_EG + G * P


def constants():
    c = np.zeros((P, C_END), np.float32)
    p = np.arange(P)
    c[:, C_ID:C_ID + P] = np.eye(P)
    c[:, C_UT:C_UT + P] = p[:, None] <= p[None, :]
    c[:, C_ONE:C_ONE + P] = 1.0
    c[:, C_TRI:C_TRI + P] = p[:, None] > p[None, :]
    for j in range(J):
        c[:, C_MQ + j] = (p // HD % J == j) * np.float32(1 / np.sqrt(np.float32(HD)))
        c[:, C_MK + j] = p // (J * HD) == j
        c[:, C_MM + j] = p % (J * HD) == j
        c[:, C_EG + j * P:C_EG + (j + 1) * P] = (p // (J * HD) == j)[:, None]
    return c


def wait(eng, sem, value):
    if not isinstance(value, int) or value > 0:
        eng.wait_ge(sem, value)


class Chain:

    def __init__(self, eng, sem):
        self.eng, self.sem, self.base, self.k, self.past = eng, sem, 0, 0, 0

    def __call__(self, ins):
        self.k += 1
        ins.then_inc(self.sem, 1)
        self.eng.wait_ge(self.sem, self.past + (self.base + self.k))

    def before(self, passed, links):
        self.base, self.k = self.base + self.k, 0
        self.past = passed * links

    def after(self, passes, links):
        assert self.k == links, (self.k, links)
        self.base, self.k, self.past = self.base + links * passes, 0, 0


def tile_of(X, t):
    return X[:, bass.ds(t, 1), :].rearrange("p a n -> p (a n)")


def build(nc, a, out):
    with ExitStack() as ctx:
        def sb(name, shape, dt=F32):
            return ctx.enter_context(nc.sbuf_tensor(name, shape, dt))

        def sem(name):
            return ctx.enter_context(nc.semaphore(name))

        psum = [ctx.enter_context(nc.psum_tensor(f"bank{i}", [P, 512], F32)) for i in range(8)]

        X = sb("X", [P, TILES, P])
        cst = sb("cst", [P, C_END])
        ident = cst[:, C_ID:C_ID + P]
        upper = cst[:, C_UT:C_UT + P]
        ones = cst[:, C_ONE:C_ONE + P]
        ident_b = sb("ident_b", [P, P], BF16)
        tri_b = sb("tri_b", [P, J, P], BF16)
        eg_b = sb("eg_b", [P, G, P], BF16)
        half = sb("half", [P, GT])
        eps = sb("eps", [P, GT])

        loads = []

        def load(name, shape, src):
            t = sb(name, shape)
            loads.append((t[:], src))
            return t

        loads.append((cst[:], a["cst"]))
        projT = [load(f"projT{b}", [P, P], a[f"projT{b}"]) for b in range(2)]
        winT = [load(f"winT{b}", [P, 3 * P], a[f"winT{b}"]) for b in range(2)]
        woutT = [load(f"woutT{b}", [P, P], a[f"woutT{b}"]) for b in range(2)]
        bq = [load(f"bq{b}", [P, 3], a[f"bcol{b}"]) for b in range(2)]
        bv = [load(f"bv{b}", [P, P], a[f"bin{b}"][2 * P:3 * P].partition_broadcast(P)) for b in range(2)]
        bout = [load(f"bout{b}", [P, P], a[f"bout{b}"].partition_broadcast(P)) for b in range(2)]
        fw = load("fw", [P, 2], a["fusion"].partition_broadcast(P))
        gamma = load("gamma", [P, P], a["gamma"].partition_broadcast(P))
        beta = load("beta", [P, P], a["beta"].partition_broadcast(P))
        wrT = load("wrT", [P, P], a["wrT"])
        wkT = load("wkT", [P, P], a["wkT"])
        wvT = load("wvT", [P, P], a["wvT"])
        mu = load("mu", [P, 2], a["mu"])
        wqkvT = sb("wqkvT", [P, 3, P])
        bqkv = sb("bqkv", [P, 3, P])
        for i, n in enumerate("qkv"):
            loads.append((wqkvT[:, i, :], a[f"lw{n}T"]))
            loads.append((bqkv[:, i, :], a[f"lb{n}"].partition_broadcast(P)))
        woT = load("woT", [P, P], a["lwoT"])
        bo = load("bo", [P, P], a["lbo"].partition_broadcast(P))
        w1T = load("w1T", [P, HIDDEN], a["w1T"])
        w2T = load("w2T", [P, HIDDEN], a["w2T"])
        h1T = load("h1T", [P, HC, HIDDEN], a["h1T"].rearrange("(c p) n -> p c n", p=P))
        h2T = load("h2T", [P, HC, HIDDEN], a["h2T"].rearrange("(c p) n -> p c n", p=P))
        w3T = load("w3T", [P, HC, P], a["w3T"].rearrange("(c p) n -> p c n", p=P))
        scol = load("scol", [P, 4, HC], a["scol"])
        s3 = load("s3", [P, P], a["w3_s"].partition_broadcast(P))

        weights_in, x_in, consts_ready = sem("weights_in"), sem("x_in"), sem("consts_ready")
        setup_pe, setup_act, setup_dve = sem("setup_pe"), sem("setup_act"), sem("setup_dve")
        dve_own, pool_own, act_own = sem("dve_own"), sem("pool_own"), sem("act_own")
        stored = sem("stored")

        x_tok = a["x"].rearrange("(t p) n -> p t n", p=P)
        xT_win = a["xT"].rearrange("p (t n) -> p t n", n=P)
        out_tok = out.rearrange("(t p) n -> p t n", p=P)

        wcT = [sb(f"wcT{b}", [P, 3 * P]) for b in range(2)]
        wos = [sb(f"wos{b}", [P, P]) for b in range(2)]
        fbias = sb("fbias", [P, P])
        fsm = sb("fsm", [P, 8])
        omu = sb("omu", [P, 2])
        h1s = sb("h1s", [P, HC, HIDDEN])
        w3s = sb("w3s", [P, HC, P])
        halfs = sb("halfs", [P, 2, HC])
        fb1 = sb("fb1", [P, P])

        xTw = sb("xTw", [P, P])
        qx = [sb(f"qx{i}", [P, J, P]) for i in range(2)]
        kz = [sb(f"kz{i}", [P, G, P]) for i in range(2)]
        qxb = [sb(f"qxb{i}", [P, J, P], BF16) for i in range(2)]
        kzb = [sb(f"kzb{i}", [P, G, P], BF16) for i in range(2)]
        va = [sb(f"va{i}", [P, HEADS, NE]) for i in range(2)]
        mx = [sb(f"mx{i}", [P, P], BF16) for i in range(2)]
        mxx = [sb(f"mxx{i}", [P, J, P], BF16) for i in range(2)]
        probs = sb("probs", [P, 2, G, J * P])
        pr = [[probs[:, i, g, :].rearrange("p (j q) -> p j q", j=J) for g in range(G)] for i in range(2)]
        rec = [sb(f"rec{i}", [P, HEADS]) for i in range(2)]
        on = [sb(f"on{i}", [P, P]) for i in range(2)]
        onT = [sb(f"onT{i}", [P, P]) for i in range(2)]
        fused = sb("fused", [P, P])
        st6 = sb("st6", [P, GT, 6])
        mv = sb("mv", [P, GT, 2])
        mv2 = sb("mv2", [P, GT, 2])
        rs = sb("rs", [P, GT])
        rs2 = sb("rs2", [P, GT])
        z1 = sb("z1", [P, P])
        mvp = [sb(f"mvp{i}", [P, GT, 2]) for i in range(2)]

        xT_in = sem("xT_in")
        qkv_done, qkv_read = sem("qkv_done"), sem("qkv_read")
        q_ready, k_ready, bf_ready = sem("q_ready"), sem("k_ready"), sem("bf_ready")
        mq_done, max_ready = sem("mq_done"), sem("max_ready")
        mT_done, mxx_ready = sem("mT_done"), sem("mxx_ready")
        s_done, probs_ready = sem("s_done"), sem("probs_ready")
        o_done, on_ready = sem("o_done"), sem("on_ready")
        oT_done, onT_ready = sem("oT_done"), sem("onT_ready")
        y_done, y_stats, y_read = sem("y_done"), sem("y_stats"), sem("y_read")
        z_ready, z_stats, x1_ready = sem("z_ready"), sem("z_stats"), sem("x1_ready")

        PJ, M, S, OB, TR, Y = psum[0], psum[1:3], psum[3:5], psum[5], psum[6], psum[7]

        xg = sb("xg", [P, GT * P])
        xs = [sb(f"xs{h}", [P, 1 + GT * P]) for h in range(2)]
        xmix = [sb(f"xmix{i}", [P, GT * P]) for i in range(2)]
        tmp = [sb(f"tmp{i}", [P, GT * P]) for i in range(2)]
        ka = sb("ka", [P, GT * P])
        th = sb("th", [P, GT * P])
        zt = [sb(f"zt{i}", [P, GT, P]) for i in range(2)]
        f_xg, f_tr, f_xs, f_mix, f_k, f_ka, f_r, f_th, f_v, f_z, f_stats, x2_ready = map(sem, (
            "f_xg", "f_tr", "f_xs", "f_mix", "f_k", "f_ka", "f_r", "f_th", "f_v", "f_z", "f_stats", "x2_ready"))

        xg3 = [sb(f"xg3{i}", [P, P]) for i in range(2)]
        xT3 = sb("xT3", [P, P])
        qkv3 = [sb(f"qkv3{i}", [P, 3, P]) for i in range(2)]
        va3 = [sb(f"va3{i}", [P, HEADS, NE]) for i in range(2)]
        mn3 = sb("mn3", [P, 2, P])
        ex3 = sb("ex3", [P, 2, P])
        phi = [sb(f"phi{i}", [P, 2, P]) for i in range(2)]
        kv = [sb(f"kv{i}", [P, HEADS, NE, HD]) for i in range(2)]
        tot = [sb(f"tot{i}", [P, HEADS, NE, HD]) for i in range(2)]
        prod = sb("prod", [P, HEADS, NE, HD])
        num = sb("num", [P, HEADS, NE])
        rec3 = sb("rec3", [P, HEADS])
        den3 = sb("den3", [P, HEADS])
        o3 = sb("o3", [P, P])
        oT3 = sb("oT3", [P, P])
        z3 = [sb(f"z3{i}", [P, P]) for i in range(2)]
        (l_xg, l_tr, l_xT, l_qkv, l_bias, l_min, l_exp, l_phi, l_kv, l_tot, l_cum, l_read, l_yread, l_o, l_oT, l_oTs,
         l_y, l_z, l_stats, x3_ready) = map(sem, (
            "l_xg", "l_tr", "l_xT", "l_qkv", "l_bias", "l_min", "l_exp", "l_phi", "l_kv", "l_tot", "l_cum", "l_read", "l_yread",
            "l_o", "l_oT", "l_oTs", "l_y", "l_z", "l_stats", "x3_ready"))

        xT4 = sb("xT4", [P, GT * P])
        th4 = [sb(f"th4{i}", [P, GT * P]) for i in range(2)]
        t4 = [sb(f"t4{i}", [P, GT * P]) for i in range(2)]
        ha = sb("ha", [P, HC, GT * P])
        hb, hc = probs[:, 0], probs[:, 1]
        (g_xg, g_tr, g_xT, g_u, g_th, g_v, g_ha, g_l1, g_hb, g_l2, g_hc, g_y, g_z, g_stats, x4_ready) = map(sem, (
            "g_xg", "g_tr", "g_xT", "g_u", "g_th", "g_v", "g_ha", "g_l1", "g_hb", "g_l2", "g_hc", "g_y", "g_z",
            "g_stats", "x4_ready"))

        block = ctx.enter_context(nc.Block())

        @block.sync
        def _(sp):
            for dst, src in loads:
                sp.dma_start(dst, src).then_inc(weights_in, 16)
            sp.dma_start(xTw[:], xT_win[:, 0, :]).then_inc(xT_in, 16)
            for b in range(BATCH):
                ts = slice(b * PER_BATCH, (b + 1) * PER_BATCH)
                sp.dma_start(X[:, ts, :], x_tok[:, ts, :]).then_inc(x_in, 16)

            with sp.Fori(1, TILES) as w:
                sp.wait_ge(qkv_done, 2 * w)
                sp.dma_start(xTw[:], xT_win[:, bass.ds(w, 1), :].rearrange("p a n -> p (a n)")).then_inc(xT_in, 16)

            with sp.Fori(0, GROUPS) as g:
                sp.wait_ge(x4_ready, g + 1)
                sp.dma_start(out_tok[:, bass.ds(g * GT, GT), :], X[:, bass.ds(g * GT, GT), :]).then_inc(stored, 16)
            sp.wait_ge(stored, 16 * GROUPS)

        @block.tensor
        def _(pe):
            pe.wait_ge(weights_in, 16 * len(loads))
            for b in range(2):
                pe.matmul(psum[b][:, 0:3 * P], projT[b][:], winT[b][:], start=True, stop=True).then_inc(setup_pe, 1)
            pe.wait_ge(consts_ready, 2)

            def project(u, b):
                if b == 0:
                    pe.wait_ge(xT_in, 8 * u + 16)
                wait(pe, qkv_read, u)
                pe.matmul(PJ[:, 0:P], wcT[b][:, 0:P], xTw[:], start=True, stop=True)
                pe.matmul(PJ[:, P:2 * P], wcT[b][:, P:2 * P], xTw[:], start=True, stop=True)
                pe.matmul(PJ[:, 2 * P:3 * P], xTw[:], wcT[b][:, 2 * P:3 * P], start=True, stop=True).then_inc(qkv_done, 1)

            def max_scores(u, b):
                pe.wait_ge(bf_ready, 2 * u + 2)
                for j in range(J):
                    wait(pe, max_ready, J * u + j - 1)
                    pe.matmul(M[j % 2][:], qxb[b][:, j, :], kzb[b][:].rearrange("p g k -> p (g k)"),
                              start=True, stop=True).then_inc(mq_done, 1)

            def turn_max(u, b):
                pe.wait_ge(max_ready, J * u + J)
                wait(pe, onT_ready, u - 1)
                pe.transpose(TR[:].bitcast(BF16)[:, 0:P], mx[b][:], ident_b[:]).then_inc(mT_done, 1)

            def scores(u, b, g):
                if g == 0:
                    pe.wait_ge(mxx_ready, u + 1)
                wait(pe, probs_ready, G * u + g - 1)
                s = S[g % 2][:]
                pe.matmul(s, kz[b][:, g, :], qx[b][:].rearrange("p j q -> p (j q)"), start=True, stop=False)
                pe.matmul(s, eg_b[:, g, :], mxx[b][:].rearrange("p j q -> p (j q)"), start=False, stop=False)
                pe.matmul(s, ident_b[:], tri_b[:].rearrange("p j q -> p (j q)"), start=False, stop=True).then_inc(s_done, 1)

            def values(u, b):
                wait(pe, on_ready, u)
                for g in range(G):
                    pe.wait_ge(probs_ready, G * u + g + 1)
                    for j in range(J):
                        h = G * g + j
                        mm = pe.matmul(OB[:, h * NE:(h + 1) * NE], pr[b][g][:, j, :], va[b][:, h, :], start=True, stop=True)
                mm.then_inc(o_done, 1)

            def turn_out(u, b):
                pe.wait_ge(on_ready, u + 1)
                pe.wait_ge(mxx_ready, u + 2)
                pe.transpose(TR[:, 0:P], on[b][:], ident).then_inc(oT_done, 1)

            def out_project(w):
                pe.wait_ge(onT_ready, 2 * w + 2)
                wait(pe, y_read, w)
                pe.matmul(Y[:, 0:P], onT[0][:], wos[0][:], start=True, stop=False)
                pe.matmul(Y[:, 0:P], onT[1][:], wos[1][:], start=False, stop=True).then_inc(y_done, 1)

            def window(w, first=False, last=False):
                for b in range(2):
                    u = 2 * w + b
                    ahead = not (last and b == 1)
                    if ahead:
                        project(u + 1, 1 - b)
                    scores(u, b, 0)
                    scores(u, b, 1)
                    if not (first and b == 0):
                        turn_out(u - 1, 1 - b)
                    if ahead:
                        max_scores(u + 1, 1 - b)
                    scores(u, b, 2)
                    scores(u, b, 3)
                    if b == 0 and not first:
                        out_project(w - 1)
                    if ahead:
                        turn_max(u + 1, 1 - b)
                    values(u, b)

            project(0, 0)
            max_scores(0, 0)
            turn_max(0, 0)
            window(0, first=True)
            with pe.Fori(1, TILES - 1) as w:
                window(w)
            window(TILES - 1, last=True)
            pe.wait_ge(on_ready, 2 * TILES)
            pe.transpose(TR[:, 0:P], on[1][:], ident).then_inc(oT_done, 1)
            out_project(TILES - 1)


            K2, R2, V2, T2 = psum[0:4]
            pe.wait_ge(x1_ready, TILES)

            def turn_x2(g):
                pe.wait_ge(f_xg, g + 1)
                wait(pe, f_xs, g)
                for t in range(GT):
                    mm = pe.transpose(T2[:, t * P:(t + 1) * P], xg[:, t * P:(t + 1) * P], ident)
                mm.then_inc(f_tr, 1)

            def shift_ffn(g, ahead=True):
                pe.wait_ge(f_mix, g + 1)
                wait(pe, f_ka, g)
                pe.matmul(K2[:], wkT[:], xmix[1][:], start=True, stop=True).then_inc(f_k, 1)
                wait(pe, f_th, g)
                for t in range(GT):
                    mm = pe.matmul(R2[:, t * P:(t + 1) * P], xmix[0][:, t * P:(t + 1) * P], wrT[:], start=True, stop=True)
                mm.then_inc(f_r, 1)
                if ahead:
                    turn_x2(g + 1)
                pe.wait_ge(f_ka, g + 1)
                wait(pe, f_z, g)
                for t in range(GT):
                    mm = pe.matmul(V2[:, t * P:(t + 1) * P], ka[:, t * P:(t + 1) * P], wvT[:], start=True, stop=True)
                mm.then_inc(f_v, 1)

            turn_x2(0)
            with pe.Fori(0, BATCH - 1) as n:
                shift_ffn(2 * n)
                shift_ffn(2 * n + 1)
            shift_ffn(GROUPS - 2)
            shift_ffn(GROUPS - 1, ahead=False)

            XO, QY, CUM = psum[0], psum[1], [psum[2:5], psum[5:8]]
            pe.wait_ge(x2_ready, GROUPS)

            def turn_x3(t, k):
                pe.wait_ge(l_xg, t + 1)
                wait(pe, l_oTs, t - 2)
                pe.transpose(XO[:, 0:P], xg3[k % 2][:], ident).then_inc(l_tr, 1)

            def project3(t):
                pe.wait_ge(l_xT, t + 1)
                wait(pe, l_yread, t - 2)
                pe.matmul(QY[:, 0:3 * P], xT3[:], wqkvT[:].rearrange("p c n -> p (c n)"),
                          start=True, stop=True).then_inc(l_qkv, 1)

            def running_sums(t, k, n, part):
                lo, hi = SPLIT[part]
                if part == 0:
                    pe.wait_ge(l_kv, t + 1)
                    wait(pe, l_read, t - 1)
                    if k >= 2:
                        pe.wait_ge(l_tot, (PER_BATCH - 2) * n + k - 1)
                bank = CUM[k % 2][part][:, 0:(hi - lo) * NE * HD]
                if k:
                    before = kv[0] if k == 1 else tot[(k - 1) % 2]
                    pe.matmul(bank, ones, before[:, lo:hi].rearrange("p h e d -> p (h e d)"), start=True, stop=False)
                mm = pe.matmul(bank, upper, kv[k % 2][:, lo:hi].rearrange("p h e d -> p (h e d)"), start=k == 0, stop=True)
                if part == 2:
                    mm.then_inc(l_cum, 1)

            def turn_o3(t, last=False):
                pe.wait_ge(l_o, t + 1)
                if last:
                    pe.wait_ge(l_oTs, t)
                pe.transpose(XO[:, 0:P], o3[:], ident).then_inc(l_oT, 1)

            def out_project3(t, last=False):
                pe.wait_ge(l_oTs, t + 1)
                if last:
                    wait(pe, l_yread, t)
                else:
                    pe.wait_ge(l_bias, t + 3)
                pe.matmul(QY[:, 0:P], oT3[:], woT[:], start=True, stop=True).then_inc(l_y, 1)

            def tile3(t, k, n, first=False, last=False):
                if not last:
                    turn_x3(t + 1, k + 1)
                running_sums(t, k, n, 0)
                if not last:
                    project3(t + 1)
                running_sums(t, k, n, 1)
                if not first:
                    turn_o3(t - 1, last)
                running_sums(t, k, n, 2)
                if not first:
                    out_project3(t - 1, last)

            def batch3(n, first=False, last=False):
                for k in range(PER_BATCH):
                    tile3(PER_BATCH * n + k, k, n, first and k == 0, last and k == PER_BATCH - 1)

            turn_x3(0, 0)
            project3(0)
            batch3(0, first=True)
            with pe.Fori(1, BATCH - 1) as n:
                batch3(n)
            batch3(BATCH - 1, last=True)
            turn_o3(TILES - 1, True)
            out_project3(TILES - 1, True)

            U4, V4, L4, T4, Y4 = psum[0:2], psum[2:4], psum[4:6], psum[6], psum[7]
            pe.wait_ge(x3_ready, TILES)

            def turn_x4(g):
                pe.wait_ge(g_xg, g + 1)
                for t in range(GT):
                    mm = pe.transpose(T4[:, t * P:(t + 1) * P], xg[:, t * P:(t + 1) * P], ident)
                mm.then_inc(g_tr, 1)

            def up(g):
                pe.wait_ge(g_xT, g + 1)
                for o in range(HC):
                    wait(pe, g_ha, HC * g + o - 1)
                    cols = slice(o * P, (o + 1) * P)
                    pe.matmul(U4[o % 2][:], w1T[:, cols], xT4[:], start=True, stop=True).then_inc(g_u, 1)
                    pe.matmul(V4[o % 2][:], w2T[:, cols], xT4[:], start=True, stop=True).then_inc(g_v, 1)

            def hidden(g, w, src, src_ready, own_ready, done):
                for o in range(HC):
                    if o >= 2:
                        pe.wait_ge(own_ready, HC * g + o - 1)
                    elif src_ready is g_hb:
                        pe.wait_ge(src_ready, HC * g + o + 3)
                    for c in range(HC):
                        if o == 0:
                            pe.wait_ge(src_ready, HC * g + c + 1)
                        mm = pe.matmul(L4[o % 2][:], w[:, c, o * P:(o + 1) * P], src[:, c, :],
                                       start=c == 0, stop=c == HC - 1)
                    mm.then_inc(done, 1)

            def down(g):
                pe.wait_ge(g_hc, HC * g + HC)
                wait(pe, g_z, g)
                for t in range(GT):
                    for c in range(HC):
                        mm = pe.matmul(Y4[:, t * P:(t + 1) * P], hc[:, c, t * P:(t + 1) * P], w3s[:, c, :],
                                       start=c == 0, stop=c == HC - 1)
                mm.then_inc(g_y, 1)

            def group4(g, first=False, last=False):
                up(g)
                if not first:
                    down(g - 1)
                hidden(g, h1s, ha, g_ha, g_hb, g_l1)
                if not last:
                    turn_x4(g + 1)
                hidden(g, h2T, hb, g_hb, g_hc, g_l2)

            turn_x4(0)
            group4(0, first=True)
            with pe.Fori(1, GROUPS - 1) as g:
                group4(g)
            group4(GROUPS - 1, last=True)
            down(GROUPS - 1)

        @block.scalar
        def _(act):
            act.wait_ge(setup_dve, 1)
            act.activation(fsm[:, 4:6], fsm[:, 2:4], ACT.Exp).then_inc(setup_act, 1)

            def exp_scores(u, b, g):
                act.wait_ge(s_done, G * u + g + 1)
                act.activation(probs[:, b, g, :], S[g % 2][:], ACT.Exp).then_inc(probs_ready, 1)

            def read_out(u, b):
                act.wait_ge(oT_done, u + 1)
                act.activation(onT[b][:], TR[:, 0:P], ACT.Copy).then_inc(onT_ready, 1)

            def round_qk(u, b):
                act.wait_ge(q_ready, u + 1)
                act.activation(qxb[b][:], qx[b][:], ACT.Copy).then_inc(bf_ready, 1)
                act.wait_ge(k_ready, u + 1)
                act.activation(kzb[b][:], kz[b][:], ACT.Copy).then_inc(bf_ready, 1)

            def window(w, first=False, last=False):
                for b in range(2):
                    u = 2 * w + b
                    exp_scores(u, b, 0)
                    if not (last and b == 1):
                        round_qk(u + 1, 1 - b)
                    exp_scores(u, b, 1)
                    if not (first and b == 0):
                        read_out(u - 1, 1 - b)
                    exp_scores(u, b, 2)
                    exp_scores(u, b, 3)

            round_qk(0, 0)
            window(0, first=True)
            with act.Fori(1, TILES - 1) as w:
                window(w)
            window(TILES - 1, last=True)
            read_out(2 * TILES - 1, 1)

            K2, R2, T2 = psum[0], psum[1], psum[3]
            own = Chain(act, act_own)
            act.wait_ge(x1_ready, TILES)

            def stage_x(g, turned, ready):
                wait(act, turned, g)
                act.activation(xg[:].rearrange("p (t n) -> p t n", t=GT), X[:, bass.ds(GT * g, GT), :], ACT.Copy).then_inc(ready, 1)

            def read_xT2(g, h):
                act.wait_ge(f_tr, g + 1)
                wait(act, f_mix, g - 1)
                if h:
                    act.activation(xs[1][:, 0:1], xs[0][:, GT * P:GT * P + 1], ACT.Copy)
                act.activation(xs[h][:, 1:1 + GT * P], T2[:], ACT.Copy).then_inc(f_xs, 1)

            def group2(g, h, ahead=True, further=True):
                act.wait_ge(f_k, g + 1)
                wait(act, f_v, g)
                own(act.activation(ka[:], K2[:], ACT.Relu))
                act.activation(ka[:], ka[:], ACT.Square).then_inc(f_ka, 1)
                if ahead:
                    read_xT2(g + 1, 1 - h)
                if further:
                    stage_x(g + 2, f_tr, f_xg)
                act.wait_ge(f_r, g + 1)
                wait(act, f_z, g)
                act.activation(th[:], R2[:], ACT.Tanh, scale=0.5).then_inc(f_th, 1)

            stage_x(0, f_tr, f_xg)
            read_xT2(0, 0)
            stage_x(1, f_tr, f_xg)
            group2(0, 0)
            group2(1, 1)
            with act.Fori(1, BATCH - 1) as n:
                own.before(n - 1, 2)
                group2(2 * n, 0)
                group2(2 * n + 1, 1)
            own.after(BATCH - 2, 2)
            group2(GROUPS - 2, 0, further=False)
            group2(GROUPS - 1, 1, ahead=False, further=False)

            XO = psum[0]
            act.wait_ge(x2_ready, GROUPS)

            def stage_x3(t, k):
                wait(act, l_tr, t - 1)
                act.activation(xg3[k % 2][:], tile_of(X, t), ACT.Copy).then_inc(l_xg, 1)

            def read_x3(t):
                act.wait_ge(l_tr, t + 1)
                wait(act, l_qkv, t)
                act.activation(xT3[:], XO[:, 0:P], ACT.Copy).then_inc(l_xT, 1)

            def exp3(t):
                act.wait_ge(l_min, t + 1)
                wait(act, l_phi, t)
                act.activation(ex3[:], mn3[:], ACT.Exp).then_inc(l_exp, 1)

            def read_o3(t):
                act.wait_ge(l_oT, t + 1)
                wait(act, l_y, t)
                act.activation(oT3[:], XO[:, 0:P], ACT.Copy).then_inc(l_oTs, 1)

            def batch3(n, first=False, last=False):
                for k in range(PER_BATCH):
                    t = PER_BATCH * n + k
                    if not (last and k == PER_BATCH - 1):
                        read_x3(t + 1)
                    if not (last and k >= PER_BATCH - 2):
                        stage_x3(t + 2, k)
                    if not (last and k == PER_BATCH - 1):
                        exp3(t + 1)
                    if not (first and k == 0):
                        read_o3(t - 1)

            stage_x3(0, 0)
            stage_x3(1, 1)
            read_x3(0)
            exp3(0)
            batch3(0, first=True)
            with act.Fori(1, BATCH - 1) as n:
                batch3(n)
            batch3(BATCH - 1, last=True)
            read_o3(TILES - 1)

            U4, L4, T4 = psum[0:2], psum[4:6], psum[6]
            act.wait_ge(x3_ready, TILES)

            def read_x4(g):
                act.wait_ge(g_tr, g + 1)
                act.activation(xT4[:], T4[:], ACT.Copy).then_inc(g_xT, 1)

            def gelu(g, dst, i, done, ready):
                for o in range(HC):
                    act.wait_ge(done, HC * g + o + 1)
                    act.activation(dst[:, o, :], L4[o % 2][:], ACT.Gelu, scale=scol[:, i, o:o + 1]).then_inc(ready, 1)

            def group4(g, last=False):
                for o in range(HC):
                    act.wait_ge(g_u, HC * g + o + 1)
                    wait(act, g_ha, HC * g + o - 1)
                    act.activation(th4[o % 2][:], U4[o % 2][:], ACT.Tanh, scale=halfs[:, 0, o:o + 1]).then_inc(g_th, 1)
                if not last:
                    stage_x(g + 1, g_tr, g_xg)
                gelu(g, hb, 2, g_l1, g_hb)
                if not last:
                    read_x4(g + 1)
                gelu(g, hc, 3, g_l2, g_hc)

            stage_x(0, g_tr, g_xg)
            read_x4(0)
            group4(0)
            with act.Fori(1, GROUPS - 1) as g:
                group4(g)
            group4(GROUPS - 1, last=True)

        @block.vector
        def _(dve):
            link = Chain(dve, dve_own)
            dve.memset(half[:], -0.5)
            dve.memset(eps[:], EPS)
            for i in range(2):
                dve.memset(va[i][:], 1.0)
                dve.memset(va3[i][:], 1.0)
                dve.memset(mx[i][:], 0.0)
            dve.memset(xs[0][:, 0:1], 0.0)
            dve.wait_ge(weights_in, 16 * len(loads))
            link(dve.tensor_reduce(fsm[:, 0:1], fw[:], AX.X, ALU.max))
            dve.tensor_scalar(fsm[:, 2:4], fw[:], fsm[:, 0:1], None, ALU.subtract).then_inc(setup_dve, 1)
            dve.tensor_copy(ident_b[:], ident)
            dve.tensor_copy(eg_b[:], cst[:, C_EG:C_END].rearrange("p (g n) -> p g n", g=G))
            dve.tensor_copy(tri_b[:], cst[:, C_TRI:C_TRI + P].unsqueeze(1).to_broadcast([P, J, P]))
            dve.tensor_scalar(omu[:], mu[:], -1.0, 1.0, ALU.mult, ALU.add)
            link(dve.tensor_tensor(halfs[:, 1, :], scol[:, 0, :], scol[:, 1, :], ALU.mult))
            dve.tensor_scalar(halfs[:, 0, :], scol[:, 0, :], 0.5, None, ALU.mult)
            link(dve.tensor_scalar(halfs[:, 1, :], halfs[:, 1, :], 0.5, None, ALU.mult))
            for c in range(HC):
                dve.tensor_scalar(h1s[:, c, :], h1T[:, c, :], halfs[:, 1, c:c + 1], None, ALU.mult)
            dve.tensor_tensor(w3s[:], w3T[:], s3[:].unsqueeze(1).to_broadcast([P, HC, P]), ALU.mult)
            dve.wait_ge(setup_act, 1)
            link(dve.tensor_reduce(fsm[:, 6:7], fsm[:, 4:6], AX.X, ALU.add))
            link(dve.reciprocal(fsm[:, 7:8], fsm[:, 6:7]))
            link(dve.tensor_scalar(fsm[:, 0:2], fsm[:, 4:6], fsm[:, 7:8], None, ALU.mult))
            for b in range(2):
                dve.tensor_scalar(wos[b][:], woutT[b][:], fsm[:, b:b + 1], None, ALU.mult)
            link(dve.tensor_scalar(fb1[:], bout[0][:], fsm[:, 0:1], None, ALU.mult))
            dve.scalar_tensor_tensor(out=fbias[:], in0=bout[1][:], scalar=fsm[:, 1:2], in1=fb1[:],
                                     op0=ALU.mult, op1=ALU.add).then_inc(consts_ready, 1)
            dve.wait_ge(setup_pe, 2)
            dve.tensor_copy(wcT[0][:], psum[0][:, 0:3 * P])
            dve.tensor_copy(wcT[1][:], psum[1][:, 0:3 * P]).then_inc(consts_ready, 1)
            dve.wait_ge(consts_ready, 2)

            def over(mask, n):
                return cst[:, mask:mask + n].unsqueeze(2).to_broadcast([P, n, P])

            def copies(bank, n):
                return bank.unsqueeze(1).to_broadcast([P, n, P])

            def read_qkv(u, b):
                dve.wait_ge(qkv_done, u + 1)
                dve.scalar_tensor_tensor(out=qx[b][:], in0=copies(PJ[:, 0:P], J), scalar=bq[b][:, 0:1],
                                         in1=over(C_MQ, J), op0=ALU.add, op1=ALU.mult).then_inc(q_ready, 1)
                dve.scalar_tensor_tensor(out=kz[b][:], in0=copies(PJ[:, P:2 * P], G), scalar=bq[b][:, 1:2],
                                         in1=over(C_MK, G), op0=ALU.add, op1=ALU.mult).then_inc(k_ready, 1)
                dve.tensor_tensor(va[b][:, :, 0:HD], PJ[:, 2 * P:3 * P].rearrange("p (h d) -> p h d", d=HD),
                                  bv[b][:].rearrange("p (h d) -> p h d", d=HD), ALU.add).then_inc(qkv_read, 1)

            def reduce_max(u, b):
                for j in range(J):
                    dve.wait_ge(mq_done, J * u + j + 1)
                    dve.tensor_reduce(mx[b][:, j:P:J * HD], M[j % 2][:].rearrange("p (g k) -> p g k", g=G),
                                      AX.X, ALU.max, negate=True).then_inc(max_ready, 1)

            def read_max(u, b):
                dve.wait_ge(mT_done, u + 1)
                dve.tensor_tensor(mxx[b][:], copies(TR[:].bitcast(BF16)[:, 0:P], J), over(C_MM, J),
                                  ALU.mult).then_inc(mxx_ready, 1)

            def normalise(u, b):
                dve.wait_ge(o_done, u + 1)
                o = OB[:, 0:HEADS * NE].rearrange("p (h e) -> p h e", e=NE)
                link(dve.reciprocal(rec[b][:].unsqueeze(2), o[:, :, HD:NE]))
                dve.tensor_tensor(on[b][:].rearrange("p (h d) -> p h d", d=HD), o[:, :, 0:HD],
                                  rec[b][:].unsqueeze(2).to_broadcast([P, HEADS, HD]), ALU.mult).then_inc(on_ready, 1)

            def fuse(w):
                dve.wait_ge(y_done, w + 1)
                wait(dve, x1_ready, w)
                dve.tensor_tensor(fused[:], Y[:, 0:P], fbias[:], ALU.add).then_inc(y_read, 1)
                dve.wait_ge(y_read, w + 1)
                dve.bn_stats(st6[:, 0, :], fused[:])
                dve.drain()
                dve.bn_aggr(mv[:, 0, :], st6[:, 0, :]).then_inc(y_stats, 1)

            def residual_stats(w):
                dve.wait_ge(z_ready, w + 1)
                dve.bn_stats(st6[:, 1, :], z1[:])
                dve.drain()
                dve.bn_aggr(mv2[:, 0, :], st6[:, 1, :]).then_inc(z_stats, 1)

            def window(w, first=False, last=False):
                for b in range(2):
                    u = 2 * w + b
                    ahead = not (last and b == 1)
                    if ahead:
                        read_qkv(u + 1, 1 - b)
                        reduce_max(u + 1, 1 - b)
                    if not first:
                        if b == 0:
                            fuse(w - 1)
                        else:
                            residual_stats(w - 1)
                    if ahead:
                        read_max(u + 1, 1 - b)
                    normalise(u, b)

            read_qkv(0, 0)
            reduce_max(0, 0)
            read_max(0, 0)
            window(0, first=True)
            LINKS = 2
            with dve.Fori(1, TILES - 1) as w:
                link.before(w - 1, LINKS)
                window(w)
            link.after(TILES - 2, LINKS)
            window(TILES - 1, last=True)
            fuse(TILES - 1)
            residual_stats(TILES - 1)

            V2 = psum[2]

            def statistics(z, m, count, done):
                for t in range(count):
                    dve.bn_stats(st6[:, t, :], z[:, t, :])
                dve.drain()
                for t in range(count):
                    last = dve.bn_aggr(m[:, t, :], st6[:, t, :])
                last.then_inc(done, 1)

            def mix(g, h):
                dve.wait_ge(f_xs, g + 1)
                wait(dve, f_r, g)
                for i in range(2):
                    last = dve.tensor_scalar(tmp[i][:], xs[h][:, 0:GT * P], omu[:, i:i + 1], None, ALU.mult)
                link(last)
                for i in range(2):
                    last = dve.scalar_tensor_tensor(out=xmix[i][:], in0=xs[h][:, 1:1 + GT * P], scalar=mu[:, i:i + 1],
                                                    in1=tmp[i][:], op0=ALU.mult, op1=ALU.add)
                last.then_inc(f_mix, 1)

            def group2(g, h, ahead=True):
                if ahead:
                    mix(g + 1, 1 - h)
                dve.wait_ge(f_v, g + 1)
                dve.wait_ge(f_th, g + 1)
                wait(dve, x2_ready, g - 1)
                z = zt[h][:]
                dve.scalar_tensor_tensor(out=z.rearrange("p t n -> p (t n)"), in0=th[:], scalar=1.0, in1=V2[:],
                                         op0=ALU.add, op1=ALU.mult).then_inc(f_z, 1)
                dve.wait_ge(f_z, g + 1)
                link(dve.scalar_tensor_tensor(out=z, in0=z, scalar=0.5, in1=X[:, bass.ds(GT * g, GT), :],
                                              op0=ALU.mult, op1=ALU.add))
                statistics(z, mvp[h], GT, f_stats)

            mix(0, 0)
            group2(0, 0)
            group2(1, 1)
            LINKS = 4
            with dve.Fori(1, BATCH - 1) as n:
                link.before(n - 1, LINKS)
                group2(2 * n, 0)
                group2(2 * n + 1, 1)
            link.after(BATCH - 2, LINKS)
            group2(GROUPS - 2, 0)
            group2(GROUPS - 1, 1, ahead=False)

            QY, CUM = psum[1], [psum[2:5], psum[5:8]]

            def features(t, k):
                dve.wait_ge(l_qkv, t + 1)
                wait(dve, l_kv, t - 1)
                i = k % 2
                dve.tensor_tensor(qkv3[i][:, 0:2, :], QY[:, 0:2 * P].rearrange("p (c n) -> p c n", c=2),
                                  bqkv[:, 0:2, :], ALU.add)
                dve.tensor_tensor(va3[i][:, :, 0:HD], QY[:, 2 * P:3 * P].rearrange("p (h d) -> p h d", d=HD),
                                  bqkv[:, 2, :].rearrange("p (h d) -> p h d", d=HD), ALU.add).then_inc(l_bias, 1)
                dve.wait_ge(l_bias, t + 1)
                dve.tensor_scalar(mn3[:], qkv3[i][:, 0:2, :], 0.0, None, ALU.min).then_inc(l_min, 1)
                dve.wait_ge(l_exp, t + 1)
                dve.scalar_tensor_tensor(out=phi[i][:], in0=qkv3[i][:, 0:2, :], scalar=0.0, in1=ex3[:],
                                         op0=ALU.max, op1=ALU.add).then_inc(l_phi, 1)

            def attend(t, k):
                i = k % 2
                dve.wait_ge(l_cum, t + 1)
                dve.wait_ge(l_phi, t + 1)
                for (lo, hi), bank in zip(SPLIT, CUM[i]):
                    n = hi - lo
                    q = phi[i][:, 0, lo * HD:hi * HD].rearrange("p (h d) -> p h d", d=HD)
                    last = dve.tensor_tensor(prod[:, lo:hi], bank[:, 0:n * NE * HD].rearrange("p (h e d) -> p h e d", e=NE, d=HD),
                                             q.unsqueeze(2).to_broadcast([P, n, NE, HD]), ALU.mult)
                last.then_inc(l_read, 1)
                dve.wait_ge(l_read, t + 1)
                link(dve.tensor_reduce(num[:], prod[:], AX.X, ALU.add))
                link(dve.tensor_scalar(den3[:].unsqueeze(2), num[:, :, HD:NE], EPS_LINEAR, None, ALU.add))
                link(dve.reciprocal(rec3[:], den3[:]))
                wait(dve, l_oT, t)
                dve.tensor_tensor(o3[:].rearrange("p (h d) -> p h d", d=HD), num[:, :, 0:HD],
                                  rec3[:].unsqueeze(2).to_broadcast([P, HEADS, HD]), ALU.mult).then_inc(l_o, 1)

            def residual3(t, k):
                dve.wait_ge(l_y, t + 1)
                wait(dve, x3_ready, t - 1)
                i = k % 2
                dve.tensor_tensor(z3[i][:], QY[:, 0:P], bo[:], ALU.add).then_inc(l_yread, 1)
                dve.wait_ge(l_yread, t + 1)
                link(dve.tensor_tensor(z3[i][:], z3[i][:], tile_of(X, t), ALU.add))
                statistics(z3[i][:].unsqueeze(1), mvp[i], 1, l_stats)

            def batch3(n, first=False, last=False):
                for k in range(PER_BATCH):
                    t = PER_BATCH * n + k
                    if not (last and k == PER_BATCH - 1):
                        features(t + 1, k + 1)
                    attend(t, k)
                    if not (first and k == 0):
                        residual3(t - 1, k - 1)

            features(0, 0)
            batch3(0, first=True)
            LINKS = 4 * PER_BATCH
            with dve.Fori(1, BATCH - 1) as n:
                link.before(n - 1, LINKS)
                batch3(n)
            link.after(BATCH - 2, LINKS)
            batch3(BATCH - 1, last=True)
            residual3(TILES - 1, PER_BATCH - 1)

            U4, V4, Y4 = psum[0:2], psum[2:4], psum[7]

            def gate(g):
                for o in range(HC):
                    i = o % 2
                    dve.wait_ge(g_th, HC * g + o + 1)
                    link(dve.scalar_tensor_tensor(out=t4[i][:], in0=th4[i][:], scalar=1.0, in1=U4[i][:],
                                                  op0=ALU.add, op1=ALU.mult))
                    dve.wait_ge(g_v, HC * g + o + 1)
                    dve.tensor_tensor(ha[:, o, :], t4[i][:], V4[i][:], ALU.mult).then_inc(g_ha, 1)

            def residual4(g):
                dve.wait_ge(g_y, g + 1)
                wait(dve, x4_ready, g)
                dve.tensor_tensor(zt[0][:], Y4[:].rearrange("p (t n) -> p t n", t=GT),
                                  X[:, bass.ds(GT * g, GT), :], ALU.add).then_inc(g_z, 1)
                dve.wait_ge(g_z, g + 1)
                statistics(zt[0][:], mvp[0], GT, g_stats)

            gate(0)
            LINKS = HC
            with dve.Fori(1, GROUPS) as g:
                link.before(g - 1, LINKS)
                gate(g)
                residual4(g - 1)
            link.after(GROUPS - 1, LINKS)
            residual4(GROUPS - 1)

        @block.gpsimd
        def _(pool):
            link = Chain(pool, pool_own)
            pool.wait_ge(x_in, 16 * BATCH)
            pool.wait_ge(consts_ready, 2)

            def inverse_std(r, m, count):
                link(pool.tensor_tensor(r[:, 0:count].unsqueeze(2), m[:, 0:count, 1:2], eps[:, 0:count].unsqueeze(2), ALU.add))
                link(pool.tensor_tensor(r[:, 0:count], r[:, 0:count], half[:, 0:count], ALU.pow))

            def spread(col):
                return col.unsqueeze(2).to_broadcast([P, col.shape[1], P])

            def inner_norm(w):
                pool.wait_ge(y_stats, w + 1)
                inverse_std(rs, mv, 1)
                link(pool.tensor_tensor(z1[:], fused[:], mv[:, 0, 0:1].to_broadcast([P, P]), ALU.subtract))
                link(pool.tensor_tensor(z1[:], z1[:], rs[:, 0:1].to_broadcast([P, P]), ALU.mult))
                link(pool.tensor_tensor(z1[:], z1[:], gamma[:], ALU.mult))
                pool.tensor_tensor(z1[:], z1[:], beta[:], ALU.add)
                pool.drain()
                pool.tensor_tensor(z1[:], z1[:], tile_of(X, w), ALU.add).then_inc(z_ready, 1)

            def outer_norm(w):
                pool.wait_ge(z_stats, w + 1)
                inverse_std(rs2, mv2, 1)
                pool.tensor_tensor(z1[:], z1[:], mv2[:, 0, 0:1].to_broadcast([P, P]), ALU.subtract)
                pool.drain()
                pool.tensor_tensor(tile_of(X, w), z1[:], rs2[:, 0:1].to_broadcast([P, P]), ALU.mult).then_inc(x1_ready, 1)

            LINKS = 7
            with pool.Fori(1, TILES - 1) as w:
                link.before(w - 1, LINKS)
                inner_norm(w - 1)
                outer_norm(w - 1)
            link.after(TILES - 2, LINKS)
            for w in (TILES - 2, TILES - 1):
                inner_norm(w)
                outer_norm(w)

            def norm(stats, ready, n, z, m, first_tile, count):
                pool.wait_ge(stats, n + 1)
                inverse_std(rs, m, count)
                pool.tensor_tensor(z, z, spread(m[:, 0:count, 0]), ALU.subtract)
                pool.drain()
                pool.tensor_tensor(X[:, bass.ds(first_tile, count), :], z, spread(rs[:, 0:count]), ALU.mult).then_inc(ready, 1)
                pool.wait_ge(ready, n + 1)

            with pool.Fori(0, BATCH) as n:
                link.before(n, 4)
                for h in range(2):
                    norm(f_stats, x2_ready, 2 * n + h, zt[h][:], mvp[h], (2 * n + h) * GT, GT)
            link.after(BATCH, 4)

            def products(t, k, n):
                pool.wait_ge(l_phi, t + 1)
                if k in (0, 2):
                    wait(pool, l_tot, TOTALS * n + k // 2)
                wait(pool, l_cum, t if k == 2 else t - 1)
                pool.tensor_tensor(kv[k % 2][:], va3[k % 2][:].unsqueeze(3).to_broadcast([P, HEADS, NE, HD]),
                                   phi[k % 2][:, 1, :].rearrange("p (h d) -> p h d", d=HD).unsqueeze(2)
                                   .to_broadcast([P, HEADS, NE, HD]), ALU.mult).then_inc(l_kv, 1)

            TOTALS = PER_BATCH - 2

            def total(t, k, n):
                before = kv[0] if k == 1 else tot[(k - 1) % 2]
                pool.wait_ge(l_kv, t + 1)
                wait(pool, l_tot, TOTALS * n + k - 1)
                wait(pool, l_cum, t)
                pool.tensor_tensor(tot[k % 2][:].rearrange("p h e d -> p (h e d)"), before[:].rearrange("p h e d -> p (h e d)"),
                                   kv[k % 2][:].rearrange("p h e d -> p (h e d)"), ALU.add).then_inc(l_tot, 1)

            def batch3(n, first=False, last=False):
                for k in range(PER_BATCH):
                    t = PER_BATCH * n + k
                    if 1 <= k <= PER_BATCH - 2:
                        total(t, k, n)
                    if not (last and k == PER_BATCH - 1):
                        products(t + 1, (k + 1) % PER_BATCH, n + (k + 1) // PER_BATCH)
                    if not (first and k == 0):
                        i = (k - 1) % 2
                        norm(l_stats, x3_ready, t - 1, z3[i][:].unsqueeze(1), mvp[i], t - 1, 1)

            products(0, 0, 0)
            batch3(0, first=True)
            LINKS = 2 * PER_BATCH
            with pool.Fori(1, BATCH - 1) as n:
                link.before(n - 1, LINKS)
                batch3(n)
            link.after(BATCH - 2, LINKS)
            batch3(BATCH - 1, last=True)
            norm(l_stats, x3_ready, TILES - 1, z3[1][:].unsqueeze(1), mvp[1], TILES - 1, 1)

            with pool.Fori(0, GROUPS) as g:
                link.before(g, 2)
                norm(g_stats, x4_ready, g, zt[0][:], mvp[0], GT * g, GT)
            link.after(GROUPS, 2)


def kernel(**inputs):
    from concourse import bacc
    from concourse.bass_utils import run_bass_kernel_spmd

    v = {n: np.asarray(x) for n, x in inputs.items()}
    L0, F0, L1, F1 = "L0_attn_", "L0_ffn_", "L1_attn_", "L1_ffn_"
    x = v[L0 + "x"].reshape(BATCH * SEQ, P)
    arrays = {
        "x": x, "xT": x.T, "cst": constants(),
        "projT0": v[L0 + "proj_local"].T, "projT1": v[L0 + "proj_global"].T,
        "fusion": v[L0 + "fusion_w"], "gamma": v[L0 + "ln_gamma"], "beta": v[L0 + "ln_beta"],
        "wrT": v[F0 + "W_r"].T, "wkT": v[F0 + "W_k"].T, "wvT": v[F0 + "W_v"].T,
        "mu": np.stack([v[F0 + "mu_r"], v[F0 + "mu_k"]], axis=1), "w3_s": v[F1 + "w3_s"],
        "scol": np.stack([v[F1 + n].reshape(HC, P).T for n in ("w1_s", "w2_s", "h1_s", "h2_s")], axis=1),
        "w1T": v[F1 + "w1_w"].T, "w2T": v[F1 + "w2_w"].T, "w3T": v[F1 + "w3_w"].T,
        "h1T": v[F1 + "h1_w"].T, "h2T": v[F1 + "h2_w"].T,
    }
    for b, n in enumerate("lg"):
        arrays[f"winT{b}"] = v[f"{L0}W{n}_in"].T
        arrays[f"bin{b}"] = v[f"{L0}b{n}_in"]
        arrays[f"bcol{b}"] = v[f"{L0}b{n}_in"].reshape(3, P).T
        arrays[f"woutT{b}"] = v[f"{L0}W{n}_out"].T
        arrays[f"bout{b}"] = v[f"{L0}b{n}_out"]
    for n in "qkvo":
        arrays[f"lw{n}T"] = v[f"{L1}W{n}"].T
        arrays[f"lb{n}"] = v[f"{L1}b{n}"]
    arrays = {n: np.ascontiguousarray(t) for n, t in arrays.items()}

    nc = bacc.Bacc("TRN2", target_bir_lowering=False, num_devices=1)
    dram = {n: nc.dram_tensor(f"in_{n}", t.shape, mybir.dt.from_np(t.dtype), kind="ExternalInput").ap()
            for n, t in arrays.items()}
    out = nc.dram_tensor("out_y", [BATCH * SEQ, P], F32, kind="ExternalOutput").ap()
    build(nc, dram, out)
    r = run_bass_kernel_spmd(nc, [{f"in_{n}": t for n, t in arrays.items()}], core_ids=[0])
    return r.results[0]["out_y"].reshape(BATCH, SEQ, P)
```

```python
from contextlib import ExitStack

import numpy as np

import concourse.bass as bass
from concourse import mybir

F32 = mybir.dt.float32
BF16 = mybir.dt.bfloat16
F16 = mybir.dt.float16
F32R = mybir.dt.float32r
ALU = mybir.AluOpType
ACT = mybir.ActivationFunctionType
AX = mybir.AxisListType

P = 128
BATCH, SEQ = 8, 1024
TILES = BATCH * SEQ // P
UNITS = 2 * TILES
PER_BATCH = SEQ // P
HEADS, HD = 16, 8
J = 4
G = HEADS // J
HIDDEN = 512
HC = HIDDEN // P
GT = 4
GROUPS = TILES // GT
NE = HD + 1
EPS = 1e-5
EPS_LINEAR = 1e-6
VP = 3
NV = VP * HD + 1
SHIFT = 4.875
SPLIT = [(0, 6), (6, 11), (11, 16)]

C_ID, C_UT, C_LT, C_ONE, C_TRI = 0, P, 2 * P, 3 * P, 4 * P
C_MQ = C_TRI + P
C_MK = C_MQ + J
C_MM = C_MK + G
C_EG = C_MM + J
C_END = C_EG + G * P


def constants():
    c = np.zeros((P, C_END), np.float32)
    p = np.arange(P)
    c[:, C_ID:C_ID + P] = np.eye(P)
    c[:, C_UT:C_UT + P] = p[:, None] <= p[None, :]
    c[:, C_LT:C_LT + P] = p[:, None] > p[None, :]
    c[:, C_ONE:C_ONE + P] = 1.0
    c[:, C_TRI:C_TRI + P] = SHIFT + (p[:, None] > p[None, :])
    for j in range(J):
        c[:, C_MQ + j] = (p // HD % J == j) * np.float32(1 / np.sqrt(np.float32(HD)))
        c[:, C_MK + j] = p // (J * HD) == j
        c[:, C_MM + j] = (p % (J * HD) < 2 * HD) & (p % HD == j)
        c[:, C_EG + j * P:C_EG + (j + 1) * P] = (p // (J * HD) == j)[:, None]
    return c


def wait(eng, sem, value):
    if not isinstance(value, int) or value > 0:
        eng.wait_ge(sem, value)


class Chain:

    def __init__(self, eng, sem):
        self.eng, self.sem, self.base, self.k, self.past = eng, sem, 0, 0, 0

    def __call__(self, ins):
        self.k += 1
        ins.then_inc(self.sem, 1)
        self.eng.wait_ge(self.sem, self.past + (self.base + self.k))

    def before(self, passed, links):
        self.base, self.k = self.base + self.k, 0
        self.past = passed * links

    def after(self, passes, links):
        assert self.k == links, (self.k, links)
        self.base, self.k, self.past = self.base + links * passes, 0, 0


def there(t, count=TILES):
    return not isinstance(t, int) or 0 <= t < count


def windows(eng, steps, chain=None, links=0):
    for w in (-1, 0, 1):
        steps(w)
    with eng.Fori(2, TILES - 1) as w:
        if chain:
            chain.before(w - 2, links)
        steps(w)
    if chain:
        chain.after(TILES - 3, links)
    for w in (TILES - 1, TILES, TILES + 1):
        steps(w)


def tile_of(X, t):
    return X[:, bass.ds(t, 1), :].rearrange("p a n -> p (a n)")


def build(nc, a, out):
    with ExitStack() as ctx:
        def sb(name, shape, dt=F32):
            return ctx.enter_context(nc.sbuf_tensor(name, shape, dt))

        def sem(name):
            return ctx.enter_context(nc.semaphore(name))

        psum = [ctx.enter_context(nc.psum_tensor(f"bank{i}", [P, 512], F32)) for i in range(8)]

        X = sb("X", [P, TILES, P])
        cst = sb("cst", [P, C_END])
        ident = cst[:, C_ID:C_ID + P]
        upper = cst[:, C_UT:C_UT + P]
        lower = cst[:, C_LT:C_LT + P]
        ones = cst[:, C_ONE:C_ONE + P]
        ident_b = sb("ident_b", [P, P], BF16)
        tri_b = sb("tri_b", [P, J, P], BF16)
        eg_b = sb("eg_b", [P, G, P], BF16)
        half = sb("half", [P, GT])
        eps = sb("eps", [P, GT])

        loads = []

        def load(name, shape, src):
            t = sb(name, shape)
            loads.append((t[:], src))
            return t

        loads.append((cst[:], a["cst"]))
        projT = [load(f"projT{b}", [P, P], a[f"projT{b}"]) for b in range(2)]
        winT = [load(f"winT{b}", [P, 3 * P], a[f"winT{b}"]) for b in range(2)]
        woutT = [load(f"woutT{b}", [P, P], a[f"woutT{b}"]) for b in range(2)]
        bq = [load(f"bq{b}", [P, 3], a[f"bcol{b}"]) for b in range(2)]
        bv = [load(f"bv{b}", [P, P], a[f"bin{b}"][2 * P:3 * P].partition_broadcast(P)) for b in range(2)]
        bout = [load(f"bout{b}", [P, P], a[f"bout{b}"].partition_broadcast(P)) for b in range(2)]
        fw = load("fw", [P, 2], a["fusion"].partition_broadcast(P))
        gamma = load("gamma", [P, P], a["gamma"].partition_broadcast(P))
        beta = load("beta", [P, P], a["beta"].partition_broadcast(P))
        wrT = load("wrT", [P, P], a["wrT"])
        wkT = load("wkT", [P, P], a["wkT"])
        wvT = load("wvT", [P, P], a["wvT"])
        mu = load("mu", [P, 2], a["mu"])
        wqkvT = sb("wqkvT", [P, 3, P])
        bqkv = sb("bqkv", [P, 3, P])
        for i, n in enumerate("qkv"):
            loads.append((wqkvT[:, i, :], a[f"lw{n}T"]))
            loads.append((bqkv[:, i, :], a[f"lb{n}"].partition_broadcast(P)))
        woT = load("woT", [P, P], a["lwoT"])
        bo = load("bo", [P, P], a["lbo"].partition_broadcast(P))
        w1T = load("w1T", [P, HIDDEN], a["w1T"])
        w2T = load("w2T", [P, HIDDEN], a["w2T"])
        h1T = load("h1T", [P, HC, HIDDEN], a["h1T"].rearrange("(c p) n -> p c n", p=P))
        h2T = load("h2T", [P, HC, HIDDEN], a["h2T"].rearrange("(c p) n -> p c n", p=P))
        w3T = load("w3T", [P, HC, P], a["w3T"].rearrange("(c p) n -> p c n", p=P))
        scol = load("scol", [P, 4, HC], a["scol"])
        s3 = load("s3", [P, P], a["w3_s"].partition_broadcast(P))

        weights_in, x_in, consts_ready = sem("weights_in"), sem("x_in"), sem("consts_ready")
        setup_pe, setup_act, setup_dve = sem("setup_pe"), sem("setup_act"), sem("setup_dve")
        dve_own, pool_own, act_own = sem("dve_own"), sem("pool_own"), sem("act_own")
        stored = sem("stored")

        x_tok = a["x"].rearrange("(t p) n -> p t n", p=P)
        xT_win = a["xT"].rearrange("p (t n) -> p t n", n=P)
        out_tok = out.rearrange("(t p) n -> p t n", p=P)

        wcT = [sb(f"wcT{b}", [P, 3 * P]) for b in range(2)]
        wos = [sb(f"wos{b}", [P, P]) for b in range(2)]
        fbias = sb("fbias", [P, P])
        fsm = sb("fsm", [P, 8])
        omu = sb("omu", [P, 2])
        h1s = sb("h1s", [P, HC, HIDDEN])
        w3s = sb("w3s", [P, HC, P])
        halfs = sb("halfs", [P, 2, HC])
        fb1 = sb("fb1", [P, P])

        st6 = sb("st6", [P, GT, 6])
        rs = sb("rs", [P, GT])
        mvp = [sb(f"mvp{i}", [P, GT, 2]) for i in range(2)]
        xg = sb("xg", [P, GT * P])
        zt = [sb(f"zt{i}", [P, GT, P]) for i in range(2)]

        own_stage = ctx.enter_context(ExitStack())

        def st(name, shape, dt=F32):
            return own_stage.enter_context(nc.sbuf_tensor(name, shape, dt))

        xTw = st("xTw", [P, P])
        qx = [st(f"qx{i}", [P, J, P]) for i in range(2)]
        kz = [st(f"kz{i}", [P, G, P]) for i in range(2)]
        qxb = [st(f"qxb{i}", [P, J, P], F32R) for i in range(2)]
        kzb = [st(f"kzb{i}", [P, G, P], F32R) for i in range(2)]
        v32 = [st(f"v32{i}", [P, HEADS, HD]) for i in range(2)]
        vr = st("vr", [P, HEADS, HD])
        vs = [st(f"vs{i}", [P, HEADS, NV], BF16) for i in range(2)]
        m32 = [st(f"m32{i}", [P, J, G]) for i in range(2)]
        mx = [st(f"mx{i}", [P, P], BF16) for i in range(2)]
        mxx = [st(f"mxx{i}", [P, J, P], BF16) for i in range(2)]
        probs = st("probs", [P, 2, G, J * P])
        pr = [[probs[:, i, g, :].rearrange("p (j q) -> p j q", j=J) for g in range(G)] for i in range(2)]
        prh = st("prh", [P, 2, G, J * P], F16)
        prl = st("prl", [P, 2, G, J * P], F16)
        osum = [st(f"osum{i}", [P, HEADS, HD]) for i in range(2)]
        rec = [st(f"rec{i}", [P, HEADS]) for i in range(2)]
        on = [st(f"on{i}", [P, P]) for i in range(2)]
        onT = [st(f"onT{i}", [P, P]) for i in range(2)]
        fused = st("fused", [P, P])
        mv = st("mv", [P, GT, 2])
        mv2 = st("mv2", [P, GT, 2])
        rs2 = st("rs2", [P, GT])
        z1 = st("z1", [P, P])

        xT_in = sem("xT_in")
        qkv_done, qkv_read = sem("qkv_done"), sem("qkv_read")
        q_ready, k_ready, bf_ready = sem("q_ready"), sem("k_ready"), sem("bf_ready")
        v_ready, m_reduced, lo_ready = sem("v_ready"), sem("m_reduced"), [sem("lo_pool"), sem("lo_dve")]
        high_ready = sem("high_ready")
        mq_done, max_ready = sem("mq_done"), sem("max_ready")
        mT_done, mxx_ready = sem("mT_done"), sem("mxx_ready")
        s_done, probs_ready = sem("s_done"), sem("probs_ready")
        o_done, o_read, on_ready = sem("o_done"), sem("o_read"), sem("on_ready")
        oT_done, onT_ready = sem("oT_done"), sem("onT_ready")
        y_done, y_stats, y_read = sem("y_done"), sem("y_stats"), sem("y_read")
        z_ready, z_stats, x1_ready = sem("z_ready"), sem("z_stats"), sem("x1_ready")

        PJ, M, S, OB, TR, Y = psum[0], psum[1:3], psum[3:5], psum[5], psum[6], psum[7]

        own_stage.close()
        xs = [st(f"xs{h}", [P, 1 + GT * P]) for h in range(2)]
        xmix = [st(f"xmix{i}", [P, GT * P]) for i in range(2)]
        tmp = [st(f"tmp{i}", [P, GT * P]) for i in range(2)]
        ka = st("ka", [P, GT * P])
        th = st("th", [P, GT * P])
        f_xg, f_tr, f_xs, f_mix, f_k, f_ka, f_r, f_th, f_v, f_z, f_stats, x2_ready = map(sem, (
            "f_xg", "f_tr", "f_xs", "f_mix", "f_k", "f_ka", "f_r", "f_th", "f_v", "f_z", "f_stats", "x2_ready"))

        own_stage.close()
        xg3 = [st(f"xg3{i}", [P, P]) for i in range(2)]
        xT3 = st("xT3", [P, P])
        qkv3 = [st(f"qkv3{i}", [P, 3, P]) for i in range(2)]
        va3 = [st(f"va3{i}", [P, HEADS, NE]) for i in range(4)]
        mn3 = st("mn3", [P, 2, P])
        ex3 = st("ex3", [P, 2, P])
        phi = [st(f"phi{i}", [P, 2, P]) for i in range(4)]
        kv = [st(f"kv{i}", [P, HEADS, NE, HD]) for i in range(2)]
        prod = st("prod", [P, HEADS, NE, HD])
        num = st("num", [P, HEADS, NE])
        rec3 = st("rec3", [P, HEADS])
        den3 = st("den3", [P, HEADS])
        o3 = st("o3", [P, P])
        oT3 = st("oT3", [P, P])
        z3 = [st(f"z3{i}", [P, P]) for i in range(2)]
        (l_xg, l_tr, l_xT, l_qkv, l_bias, l_min, l_exp, l_phi, l_kv, l_cum, l_read, l_yread, l_o, l_oT, l_oTs,
         l_y, l_z, l_stats, x3_ready) = map(sem, (
            "l_xg", "l_tr", "l_xT", "l_qkv", "l_bias", "l_min", "l_exp", "l_phi", "l_kv", "l_cum", "l_read", "l_yread",
            "l_o", "l_oT", "l_oTs", "l_y", "l_z", "l_stats", "x3_ready"))

        own_stage.close()
        xT4 = st("xT4", [P, GT * P])
        th4 = [st(f"th4{i}", [P, GT * P]) for i in range(2)]
        t4 = [st(f"t4{i}", [P, GT * P]) for i in range(2)]
        ha = st("ha", [P, HC, GT * P])
        hb, hc = st("hb", [P, HC, GT * P]), st("hc", [P, HC, GT * P])
        (g_xg, g_tr, g_xT, g_u, g_th, g_v, g_ha, g_l1, g_hb, g_l2, g_hc, g_y, g_z, g_stats, x4_ready) = map(sem, (
            "g_xg", "g_tr", "g_xT", "g_u", "g_th", "g_v", "g_ha", "g_l1", "g_hb", "g_l2", "g_hc", "g_y", "g_z",
            "g_stats", "x4_ready"))

        block = ctx.enter_context(nc.Block())

        @block.sync
        def _(sp):
            for dst, src in loads:
                sp.dma_start(dst, src).then_inc(weights_in, 16)
            sp.dma_start(xTw[:], xT_win[:, 0, :]).then_inc(xT_in, 16)
            for b in range(BATCH):
                ts = slice(b * PER_BATCH, (b + 1) * PER_BATCH)
                sp.dma_start(X[:, ts, :], x_tok[:, ts, :]).then_inc(x_in, 16)

            with sp.Fori(1, TILES) as w:
                sp.wait_ge(qkv_done, 2 * w)
                sp.dma_start(xTw[:], xT_win[:, bass.ds(w, 1), :].rearrange("p a n -> p (a n)")).then_inc(xT_in, 16)

            with sp.Fori(0, GROUPS) as g:
                sp.wait_ge(x4_ready, g + 1)
                sp.dma_start(out_tok[:, bass.ds(g * GT, GT), :], X[:, bass.ds(g * GT, GT), :]).then_inc(stored, 16)
            sp.wait_ge(stored, 16 * GROUPS)

        @block.tensor
        def _(pe):
            pe.wait_ge(weights_in, 16 * len(loads))
            for b in range(2):
                pe.matmul(psum[b][:, 0:3 * P], projT[b][:], winT[b][:], start=True, stop=True).then_inc(setup_pe, 1)
            pe.wait_ge(consts_ready, 2)

            def project(u, b):
                if b == 0:
                    pe.wait_ge(xT_in, 8 * u + 16)
                wait(pe, qkv_read, u)
                pe.matmul(PJ[:, 0:P], wcT[b][:, 0:P], xTw[:], start=True, stop=True)
                pe.matmul(PJ[:, P:2 * P], wcT[b][:, P:2 * P], xTw[:], start=True, stop=True)
                pe.matmul(PJ[:, 2 * P:3 * P], xTw[:], wcT[b][:, 2 * P:3 * P], start=True, stop=True).then_inc(qkv_done, 1)

            def max_scores(u, b, j):
                if j == 0:
                    pe.wait_ge(bf_ready, 2 * u + 2)
                wait(pe, m_reduced, J * u + j - 1)
                pe.matmul(M[j % 2][:], qxb[b][:, j, :], kzb[b][:].rearrange("p g k -> p (g k)"),
                          start=True, stop=True).then_inc(mq_done, 1)

            def turn_max(u, b):
                pe.wait_ge(max_ready, u + 1)
                wait(pe, onT_ready, u - 2)
                pe.transpose(TR[:].bitcast(BF16)[:, 0:P], mx[b][:], ident_b[:]).then_inc(mT_done, 1)

            def scores(u, b, g):
                if g == 0:
                    pe.wait_ge(mxx_ready, u + 1)
                wait(pe, high_ready, G * u + g - 1)
                s = S[g % 2][:]
                pe.matmul(s, kz[b][:, g, :], qx[b][:].rearrange("p j q -> p (j q)"), start=True, stop=False)
                pe.matmul(s, eg_b[:, g, :], mxx[b][:].rearrange("p j q -> p (j q)"), start=False, stop=False)
                pe.matmul(s, ident_b[:], tri_b[:].rearrange("p j q -> p (j q)"), start=False, stop=True).then_inc(s_done, 1)

            def values(u, b, g):
                if g == 0:
                    wait(pe, o_read, u)
                    pe.wait_ge(v_ready, u + 1)
                pe.wait_ge(high_ready, G * u + g + 1)
                pe.wait_ge(lo_ready[g // 2], 2 * u + g % 2 + 1)
                for j in range(J):
                    h = G * g + j
                    cols = slice(j * P, (j + 1) * P)
                    pe.matmul(OB[:, h * NV:(h + 1) * NV], prh[:, b, g, cols], vs[b][:, h, :], start=True, stop=False)
                    mm = pe.matmul(OB[:, h * NV:(h + 1) * NV], prl[:, b, g, cols], vs[b][:, h, :], start=False, stop=True)
                if g == G - 1:
                    mm.then_inc(o_done, 1)

            def turn_out(u, b):
                pe.wait_ge(on_ready, u + 1)
                pe.wait_ge(mxx_ready, u + 3 if there(u + 2, UNITS) else UNITS)
                wait(pe, onT_ready, u)
                pe.transpose(TR[:, 0:P], on[b][:], ident).then_inc(oT_done, 1)

            def out_project(w):
                pe.wait_ge(onT_ready, 2 * w + 2)
                wait(pe, y_read, w)
                pe.matmul(Y[:, 0:P], onT[0][:], wos[0][:], start=True, stop=False)
                pe.matmul(Y[:, 0:P], onT[1][:], wos[1][:], start=False, stop=True).then_inc(y_done, 1)

            def steps(w):
                for b in range(2):
                    u = 2 * w + b
                    here, next_one, before = there(u, UNITS), there(u + 1, UNITS), there(u - 1, UNITS)
                    if here:
                        scores(u, b, 0)
                    if next_one:
                        max_scores(u + 1, 1 - b, 0)
                        max_scores(u + 1, 1 - b, 1)
                    if there(u - 2, UNITS):
                        turn_out(u - 2, b)
                    if before:
                        values(u - 1, 1 - b, 2)
                    if here:
                        scores(u, b, 1)
                    if next_one:
                        max_scores(u + 1, 1 - b, 2)
                    if before:
                        values(u - 1, 1 - b, 3)
                    if there(u + 2, UNITS):
                        project(u + 2, b)
                    if here:
                        scores(u, b, 2)
                    if next_one:
                        max_scores(u + 1, 1 - b, 3)
                    if b == 1 and there(w - 1):
                        out_project(w - 1)
                    if here:
                        values(u, b, 0)
                        scores(u, b, 3)
                    if next_one:
                        turn_max(u + 1, 1 - b)
                    if here:
                        values(u, b, 1)

            windows(pe, steps)

            K2, R2, V2, T2 = psum[0:4]
            pe.wait_ge(x1_ready, TILES)

            def turn_x2(g):
                pe.wait_ge(f_xg, g + 1)
                wait(pe, f_xs, g)
                for t in range(GT):
                    mm = pe.transpose(T2[:, t * P:(t + 1) * P], xg[:, t * P:(t + 1) * P], ident)
                mm.then_inc(f_tr, 1)

            def shift_ffn(g, ahead=True):
                pe.wait_ge(f_mix, g + 1)
                wait(pe, f_ka, g)
                pe.matmul(K2[:], wkT[:], xmix[1][:], start=True, stop=True).then_inc(f_k, 1)
                wait(pe, f_th, g)
                for t in range(GT):
                    mm = pe.matmul(R2[:, t * P:(t + 1) * P], xmix[0][:, t * P:(t + 1) * P], wrT[:], start=True, stop=True)
                mm.then_inc(f_r, 1)
                if ahead:
                    turn_x2(g + 1)
                pe.wait_ge(f_ka, g + 1)
                wait(pe, f_z, g)
                for t in range(GT):
                    mm = pe.matmul(V2[:, t * P:(t + 1) * P], ka[:, t * P:(t + 1) * P], wvT[:], start=True, stop=True)
                mm.then_inc(f_v, 1)

            turn_x2(0)
            with pe.Fori(0, BATCH - 1) as n:
                shift_ffn(2 * n)
                shift_ffn(2 * n + 1)
            shift_ffn(GROUPS - 2)
            shift_ffn(GROUPS - 1, ahead=False)

            XT, QKV, SUMS, OT, Y3 = psum[0], psum[1], psum[2:5], psum[5], psum[6]
            pe.wait_ge(x2_ready, GROUPS)

            def turn_x3(t, k):
                pe.wait_ge(l_xg, t + 1)
                wait(pe, l_xT, t)
                pe.transpose(XT[:, 0:P], xg3[k % 2][:], ident).then_inc(l_tr, 1)

            def project3(t):
                pe.wait_ge(l_xT, t + 1)
                wait(pe, l_bias, t)
                pe.matmul(QKV[:, 0:3 * P], xT3[:], wqkvT[:].rearrange("p c n -> p (c n)"),
                          start=True, stop=True).then_inc(l_qkv, 1)

            def sums(t, k, part, matrix, start):
                lo, hi = SPLIT[part]
                return pe.matmul(SUMS[part][:, 0:(hi - lo) * NE * HD], matrix,
                                 kv[k % 2][:, lo:hi].rearrange("p h e d -> p (h e d)"),
                                 start=start, stop=True, skip_group_check=True)

            def upto(t, k, part):
                if part == 0:
                    pe.wait_ge(l_kv, t + 1)
                wait(pe, l_read, 3 * (t - 1) + part + 1)
                sums(t, k, part, upper, start=k == 0).then_inc(l_cum, 1)

            def behind(t, k, part):
                pe.wait_ge(l_read, 3 * t + part + 1)
                sums(t, k, part, lower, start=False)

            def turn_o3(t):
                pe.wait_ge(l_o, t + 1)
                wait(pe, l_oTs, t)
                pe.transpose(OT[:, 0:P], o3[:], ident).then_inc(l_oT, 1)

            def out_project3(t):
                pe.wait_ge(l_oTs, t + 1)
                wait(pe, l_yread, t)
                pe.matmul(Y3[:, 0:P], oT3[:], woT[:], start=True, stop=True).then_inc(l_y, 1)

            def batch3(n):
                for k in range(PER_BATCH):
                    t = PER_BATCH * n + k
                    if there(t + 2):
                        turn_x3(t + 2, k)
                    upto(t, k, 0)
                    upto(t, k, 1)
                    if there(t + 2):
                        project3(t + 2)
                    upto(t, k, 2)
                    if there(t - 1):
                        turn_o3(t - 1)
                    if k < PER_BATCH - 1:
                        for part in range(3):
                            behind(t, k, part)
                    if there(t - 1):
                        out_project3(t - 1)

            for t in range(2):
                turn_x3(t, t)
                project3(t)
            batch3(0)
            with pe.Fori(1, BATCH - 1) as n:
                batch3(n)
            batch3(BATCH - 1)
            turn_o3(TILES - 1)
            out_project3(TILES - 1)

            U4, V4, L4, T4, Y4 = psum[0:2], psum[2:4], psum[4:6], psum[6], psum[7]
            pe.wait_ge(x3_ready, TILES)

            def turn_x4(g):
                pe.wait_ge(g_xg, g + 1)
                for t in range(GT):
                    mm = pe.transpose(T4[:, t * P:(t + 1) * P], xg[:, t * P:(t + 1) * P], ident)
                mm.then_inc(g_tr, 1)

            def up(g):
                pe.wait_ge(g_xT, g + 1)
                for o in range(HC):
                    wait(pe, g_ha, HC * g + o - 1)
                    cols = slice(o * P, (o + 1) * P)
                    pe.matmul(U4[o % 2][:], w1T[:, cols], xT4[:], start=True, stop=True).then_inc(g_u, 1)
                    pe.matmul(V4[o % 2][:], w2T[:, cols], xT4[:], start=True, stop=True).then_inc(g_v, 1)

            def hidden(g, w, src, src_ready, own_ready, done):
                for o in range(HC):
                    if o >= 2:
                        pe.wait_ge(own_ready, HC * g + o - 1)
                    elif src_ready is g_hb:
                        pe.wait_ge(src_ready, HC * g + o + 3)
                    for c in range(HC):
                        if o == 0:
                            pe.wait_ge(src_ready, HC * g + c + 1)
                        mm = pe.matmul(L4[o % 2][:], w[:, c, o * P:(o + 1) * P], src[:, c, :],
                                       start=c == 0, stop=c == HC - 1)
                    mm.then_inc(done, 1)

            def down(g):
                pe.wait_ge(g_hc, HC * g + HC)
                wait(pe, g_z, g)
                for t in range(GT):
                    for c in range(HC):
                        mm = pe.matmul(Y4[:, t * P:(t + 1) * P], hc[:, c, t * P:(t + 1) * P], w3s[:, c, :],
                                       start=c == 0, stop=c == HC - 1)
                mm.then_inc(g_y, 1)

            def group4(g, first=False, last=False):
                up(g)
                if not first:
                    down(g - 1)
                hidden(g, h1s, ha, g_ha, g_hb, g_l1)
                if not last:
                    turn_x4(g + 1)
                hidden(g, h2T, hb, g_hb, g_hc, g_l2)

            turn_x4(0)
            group4(0, first=True)
            with pe.Fori(1, GROUPS - 1) as g:
                group4(g)
            group4(GROUPS - 1, last=True)
            down(GROUPS - 1)

        @block.scalar
        def _(act):
            act.wait_ge(setup_dve, 1)
            act.activation(fsm[:, 4:6], fsm[:, 2:4], ACT.Exp).then_inc(setup_act, 1)

            def exp_scores(u, b, g):
                act.wait_ge(s_done, G * u + g + 1)
                act.activation(probs[:, b, g, :], S[g % 2][:], ACT.Exp).then_inc(probs_ready, 1)
                act.activation(prh[:, b, g, :], S[g % 2][:], ACT.Exp).then_inc(high_ready, 1)

            def read_out(u, b):
                act.wait_ge(oT_done, u + 1)
                act.activation(onT[b][:], TR[:, 0:P], ACT.Copy).then_inc(onT_ready, 1)

            def round_qk(u, b):
                act.wait_ge(q_ready, u + 1)
                act.activation(qxb[b][:], qx[b][:], ACT.Copy).then_inc(bf_ready, 1)
                act.wait_ge(k_ready, u + 1)
                act.activation(kzb[b][:], kz[b][:], ACT.Copy).then_inc(bf_ready, 1)

            def steps(w):
                for b in range(2):
                    u = 2 * w + b
                    if there(u, UNITS):
                        exp_scores(u, b, 0)
                    if there(u - 2, UNITS):
                        read_out(u - 2, b)
                    if there(u, UNITS):
                        for g in range(1, G):
                            exp_scores(u, b, g)
                    if there(u + 2, UNITS):
                        round_qk(u + 2, b)

            windows(act, steps)

            K2, R2, T2 = psum[0], psum[1], psum[3]
            own = Chain(act, act_own)
            act.wait_ge(x1_ready, TILES)

            def stage_x(g, turned, ready):
                wait(act, turned, g)
                act.activation(xg[:].rearrange("p (t n) -> p t n", t=GT), X[:, bass.ds(GT * g, GT), :], ACT.Copy).then_inc(ready, 1)

            def read_xT2(g, h):
                act.wait_ge(f_tr, g + 1)
                wait(act, f_mix, g - 1)
                if h:
                    act.activation(xs[1][:, 0:1], xs[0][:, GT * P:GT * P + 1], ACT.Copy)
                act.activation(xs[h][:, 1:1 + GT * P], T2[:], ACT.Copy).then_inc(f_xs, 1)

            def group2(g, h, ahead=True, further=True):
                act.wait_ge(f_k, g + 1)
                wait(act, f_v, g)
                own(act.activation(ka[:], K2[:], ACT.Relu))
                act.activation(ka[:], ka[:], ACT.Square).then_inc(f_ka, 1)
                if ahead:
                    read_xT2(g + 1, 1 - h)
                if further:
                    stage_x(g + 2, f_tr, f_xg)
                act.wait_ge(f_r, g + 1)
                wait(act, f_z, g)
                act.activation(th[:], R2[:], ACT.Tanh, scale=0.5).then_inc(f_th, 1)

            stage_x(0, f_tr, f_xg)
            read_xT2(0, 0)
            stage_x(1, f_tr, f_xg)
            group2(0, 0)
            group2(1, 1)
            with act.Fori(1, BATCH - 1) as n:
                own.before(n - 1, 2)
                group2(2 * n, 0)
                group2(2 * n + 1, 1)
            own.after(BATCH - 2, 2)
            group2(GROUPS - 2, 0, further=False)
            group2(GROUPS - 1, 1, ahead=False, further=False)

            XT, OT = psum[0], psum[5]
            act.wait_ge(x2_ready, GROUPS)

            def stage_x3(t, k):
                wait(act, l_tr, t - 1)
                act.activation(xg3[k % 2][:], tile_of(X, t), ACT.Copy).then_inc(l_xg, 1)

            def read_x3(t):
                act.wait_ge(l_tr, t + 1)
                wait(act, l_qkv, t)
                act.activation(xT3[:], XT[:, 0:P], ACT.Copy).then_inc(l_xT, 1)

            def exp3(t):
                act.wait_ge(l_min, t + 1)
                wait(act, l_phi, t)
                act.activation(ex3[:], mn3[:], ACT.Exp).then_inc(l_exp, 1)

            def read_o3(t):
                act.wait_ge(l_oT, t + 1)
                wait(act, l_y, t)
                act.activation(oT3[:], OT[:, 0:P], ACT.Copy).then_inc(l_oTs, 1)

            def batch3(n):
                for k in range(PER_BATCH):
                    t = PER_BATCH * n + k
                    if there(t + 2):
                        read_x3(t + 2)
                    if there(t + 3):
                        stage_x3(t + 3, k + 1)
                    if there(t + 2):
                        exp3(t + 2)
                    if there(t - 1):
                        read_o3(t - 1)

            stage_x3(0, 0)
            stage_x3(1, 1)
            read_x3(0)
            stage_x3(2, 0)
            exp3(0)
            read_x3(1)
            exp3(1)
            batch3(0)
            with act.Fori(1, BATCH - 1) as n:
                batch3(n)
            batch3(BATCH - 1)
            read_o3(TILES - 1)

            U4, L4, T4 = psum[0:2], psum[4:6], psum[6]
            act.wait_ge(x3_ready, TILES)

            def read_x4(g):
                act.wait_ge(g_tr, g + 1)
                act.activation(xT4[:], T4[:], ACT.Copy).then_inc(g_xT, 1)

            def gelu(g, dst, i, done, ready):
                for o in range(HC):
                    act.wait_ge(done, HC * g + o + 1)
                    act.activation(dst[:, o, :], L4[o % 2][:], ACT.Gelu, scale=scol[:, i, o:o + 1]).then_inc(ready, 1)

            def group4(g, last=False):
                for o in range(HC):
                    act.wait_ge(g_u, HC * g + o + 1)
                    wait(act, g_ha, HC * g + o - 1)
                    act.activation(th4[o % 2][:], U4[o % 2][:], ACT.Tanh, scale=halfs[:, 0, o:o + 1]).then_inc(g_th, 1)
                if not last:
                    stage_x(g + 1, g_tr, g_xg)
                gelu(g, hb, 2, g_l1, g_hb)
                if not last:
                    read_x4(g + 1)
                gelu(g, hc, 3, g_l2, g_hc)

            stage_x(0, g_tr, g_xg)
            read_x4(0)
            group4(0)
            with act.Fori(1, GROUPS - 1) as g:
                group4(g)
            group4(GROUPS - 1, last=True)

        @block.vector
        def _(dve):
            link = Chain(dve, dve_own)
            dve.memset(half[:], -0.5)
            dve.memset(eps[:], EPS)
            for i in range(2):
                dve.memset(vs[i][:], 1.0)
                dve.memset(mx[i][:], 0.0)
            dve.wait_ge(weights_in, 16 * len(loads))
            link(dve.tensor_reduce(fsm[:, 0:1], fw[:], AX.X, ALU.max))
            dve.tensor_scalar(fsm[:, 2:4], fw[:], fsm[:, 0:1], None, ALU.subtract).then_inc(setup_dve, 1)
            dve.tensor_copy(ident_b[:], ident)
            dve.tensor_copy(eg_b[:], cst[:, C_EG:C_END].rearrange("p (g n) -> p g n", g=G))
            dve.tensor_copy(tri_b[:], cst[:, C_TRI:C_TRI + P].unsqueeze(1).to_broadcast([P, J, P]))
            dve.tensor_scalar(omu[:], mu[:], -1.0, 1.0, ALU.mult, ALU.add)
            link(dve.tensor_tensor(halfs[:, 1, :], scol[:, 0, :], scol[:, 1, :], ALU.mult))
            dve.tensor_scalar(halfs[:, 0, :], scol[:, 0, :], 0.5, None, ALU.mult)
            link(dve.tensor_scalar(halfs[:, 1, :], halfs[:, 1, :], 0.5, None, ALU.mult))
            for c in range(HC):
                dve.tensor_scalar(h1s[:, c, :], h1T[:, c, :], halfs[:, 1, c:c + 1], None, ALU.mult)
            dve.tensor_tensor(w3s[:], w3T[:], s3[:].unsqueeze(1).to_broadcast([P, HC, P]), ALU.mult)
            dve.wait_ge(setup_act, 1)
            link(dve.tensor_reduce(fsm[:, 6:7], fsm[:, 4:6], AX.X, ALU.add))
            link(dve.reciprocal(fsm[:, 7:8], fsm[:, 6:7]))
            link(dve.tensor_scalar(fsm[:, 0:2], fsm[:, 4:6], fsm[:, 7:8], None, ALU.mult))
            for b in range(2):
                dve.tensor_scalar(wos[b][:], woutT[b][:], fsm[:, b:b + 1], None, ALU.mult)
            link(dve.tensor_scalar(fb1[:], bout[0][:], fsm[:, 0:1], None, ALU.mult))
            dve.scalar_tensor_tensor(out=fbias[:], in0=bout[1][:], scalar=fsm[:, 1:2], in1=fb1[:],
                                     op0=ALU.mult, op1=ALU.add).then_inc(consts_ready, 1)
            dve.wait_ge(setup_pe, 2)
            dve.tensor_copy(wcT[0][:], psum[0][:, 0:3 * P])
            dve.tensor_copy(wcT[1][:], psum[1][:, 0:3 * P]).then_inc(consts_ready, 1)
            dve.wait_ge(consts_ready, 2)

            def over(mask, n):
                return cst[:, mask:mask + n].unsqueeze(2).to_broadcast([P, n, P])

            def copies(bank, n):
                return bank.unsqueeze(1).to_broadcast([P, n, P])

            def read_qkv(u, b):
                dve.wait_ge(qkv_done, u + 1)
                wait(dve, s_done, G * (u - 1))
                dve.scalar_tensor_tensor(out=qx[b][:], in0=copies(PJ[:, 0:P], J), scalar=bq[b][:, 0:1],
                                         in1=over(C_MQ, J), op0=ALU.add, op1=ALU.mult).then_inc(q_ready, 1)
                dve.scalar_tensor_tensor(out=kz[b][:], in0=copies(PJ[:, P:2 * P], G), scalar=bq[b][:, 1:2],
                                         in1=over(C_MK, G), op0=ALU.add, op1=ALU.mult).then_inc(k_ready, 1)
                dve.tensor_tensor(v32[b][:], PJ[:, 2 * P:3 * P].rearrange("p (h d) -> p h d", d=HD),
                                  bv[b][:].rearrange("p (h d) -> p h d", d=HD), ALU.add).then_inc(qkv_read, 1)

            def reduce_max(u, b, j):
                dve.wait_ge(mq_done, J * u + j + 1)
                dve.tensor_reduce(m32[b][:, j, :], M[j % 2][:].rearrange("p (g k) -> p g k", g=G),
                                  AX.X, ALU.max, negate=True).then_inc(m_reduced, 1)

            def split_max(u, b):
                dve.wait_ge(m_reduced, J * u + J)
                m = m32[b][:].rearrange("p j g -> p g j")
                parts = mx[b][:].rearrange("p (g r) -> p g r", g=G)
                link(dve.tensor_copy(parts[:, :, 0:J], m))
                dve.tensor_tensor(parts[:, :, HD:HD + J], m, parts[:, :, 0:J], ALU.subtract).then_inc(max_ready, 1)

            def low_part(u, b, g):
                dve.wait_ge(high_ready, G * u + g + 1)
                dve.tensor_tensor(prl[:, b, g, :], probs[:, b, g, :], prh[:, b, g, :], ALU.subtract).then_inc(lo_ready[1], 1)

            def read_max(u, b):
                dve.wait_ge(mT_done, u + 1)
                dve.tensor_tensor(mxx[b][:], copies(TR[:].bitcast(BF16)[:, 0:P], J), over(C_MM, J),
                                  ALU.mult).then_inc(mxx_ready, 1)

            def normalise(u, b):
                dve.wait_ge(o_done, u + 1)
                o = OB[:, 0:HEADS * NV].rearrange("p (h e) -> p h e", e=NV)
                dve.reciprocal(rec[b][:].unsqueeze(2), o[:, :, NV - 1:NV])
                dve.tensor_reduce(osum[b][:], o[:, :, 0:VP * HD].rearrange("p h (c d) -> p h d c", c=VP),
                                  AX.X, ALU.add).then_inc(o_read, 1)
                dve.wait_ge(o_read, u + 1)
                dve.tensor_tensor(on[b][:].rearrange("p (h d) -> p h d", d=HD), osum[b][:],
                                  rec[b][:].unsqueeze(2).to_broadcast([P, HEADS, HD]), ALU.mult).then_inc(on_ready, 1)

            def fuse(w):
                dve.wait_ge(y_done, w + 1)
                wait(dve, z_ready, w)
                dve.tensor_tensor(fused[:], Y[:, 0:P], fbias[:], ALU.add).then_inc(y_read, 1)
                dve.wait_ge(y_read, w + 1)
                dve.bn_stats(st6[:, 0, :], fused[:])
                dve.drain()
                dve.bn_aggr(mv[:, 0, :], st6[:, 0, :]).then_inc(y_stats, 1)

            def residual_stats(w):
                dve.wait_ge(z_ready, w + 1)
                dve.bn_stats(st6[:, 1, :], z1[:])
                dve.drain()
                dve.bn_aggr(mv2[:, 0, :], st6[:, 1, :]).then_inc(z_stats, 1)

            def steps(w):
                for b in range(2):
                    u = 2 * w + b
                    here, next_one, before = there(u, UNITS), there(u + 1, UNITS), there(u - 1, UNITS)
                    if next_one:
                        reduce_max(u + 1, 1 - b, 0)
                        reduce_max(u + 1, 1 - b, 1)
                    if b == 1 and there(w - 2):
                        residual_stats(w - 2)
                    if next_one:
                        reduce_max(u + 1, 1 - b, 2)
                    if before:
                        normalise(u - 1, 1 - b)
                    if next_one:
                        reduce_max(u + 1, 1 - b, 3)
                        split_max(u + 1, 1 - b)
                    if here:
                        low_part(u, b, 2)
                    if next_one:
                        read_max(u + 1, 1 - b)
                    if there(u + 2, UNITS):
                        read_qkv(u + 2, b)
                    if here:
                        low_part(u, b, 3)
                    if b == 1 and there(w - 1):
                        fuse(w - 1)

            LINKS = 2
            windows(dve, steps, link, LINKS)

            V2 = psum[2]

            def statistics(z, m, count, done):
                for t in range(count):
                    dve.bn_stats(st6[:, t, :], z[:, t, :])
                dve.drain()
                for t in range(count):
                    last = dve.bn_aggr(m[:, t, :], st6[:, t, :])
                last.then_inc(done, 1)

            def mix(g, h):
                dve.wait_ge(f_xs, g + 1)
                wait(dve, f_r, g)
                for i in range(2):
                    last = dve.tensor_scalar(tmp[i][:], xs[h][:, 0:GT * P], omu[:, i:i + 1], None, ALU.mult)
                link(last)
                for i in range(2):
                    last = dve.scalar_tensor_tensor(out=xmix[i][:], in0=xs[h][:, 1:1 + GT * P], scalar=mu[:, i:i + 1],
                                                    in1=tmp[i][:], op0=ALU.mult, op1=ALU.add)
                last.then_inc(f_mix, 1)

            def group2(g, h, ahead=True):
                if ahead:
                    mix(g + 1, 1 - h)
                dve.wait_ge(f_v, g + 1)
                dve.wait_ge(f_th, g + 1)
                wait(dve, x2_ready, g - 1)
                z = zt[h][:]
                dve.scalar_tensor_tensor(out=z.rearrange("p t n -> p (t n)"), in0=th[:], scalar=1.0, in1=V2[:],
                                         op0=ALU.add, op1=ALU.mult).then_inc(f_z, 1)
                dve.wait_ge(f_z, g + 1)
                link(dve.scalar_tensor_tensor(out=z, in0=z, scalar=0.5, in1=X[:, bass.ds(GT * g, GT), :],
                                              op0=ALU.mult, op1=ALU.add))
                statistics(z, mvp[h], GT, f_stats)

            dve.wait_ge(x1_ready, TILES)
            link(dve.memset(xs[0][:, 0:1], 0.0))
            mix(0, 0)
            group2(0, 0)
            group2(1, 1)
            LINKS = 4
            with dve.Fori(1, BATCH - 1) as n:
                link.before(n - 1, LINKS)
                group2(2 * n, 0)
                group2(2 * n + 1, 1)
            link.after(BATCH - 2, LINKS)
            group2(GROUPS - 2, 0)
            group2(GROUPS - 1, 1, ahead=False)

            QKV, SUMS, Y3 = psum[1], psum[2:5], psum[6]

            def features(t, k):
                dve.wait_ge(l_qkv, t + 1)
                wait(dve, l_kv, t - 3)
                i = k % 2
                dve.tensor_tensor(qkv3[i][:, 0:2, :], QKV[:, 0:2 * P].rearrange("p (c n) -> p c n", c=2),
                                  bqkv[:, 0:2, :], ALU.add)
                dve.tensor_tensor(va3[k % 4][:, :, 0:HD], QKV[:, 2 * P:3 * P].rearrange("p (h d) -> p h d", d=HD),
                                  bqkv[:, 2, :].rearrange("p (h d) -> p h d", d=HD), ALU.add).then_inc(l_bias, 1)
                dve.wait_ge(l_bias, t + 1)
                dve.tensor_scalar(mn3[:], qkv3[i][:, 0:2, :], 0.0, None, ALU.min).then_inc(l_min, 1)

            def elu(t, k):
                dve.wait_ge(l_exp, t + 1)
                dve.scalar_tensor_tensor(out=phi[k % 4][:], in0=qkv3[k % 2][:, 0:2, :], scalar=0.0, in1=ex3[:],
                                         op0=ALU.max, op1=ALU.add).then_inc(l_phi, 1)

            def attend(t, k, part):
                lo, hi = SPLIT[part]
                n = hi - lo
                dve.wait_ge(l_cum, 3 * t + part + 1)
                if part == 0:
                    dve.wait_ge(l_phi, t + 1)
                q = phi[k % 4][:, 0, lo * HD:hi * HD].rearrange("p (h d) -> p h d", d=HD)
                dve.tensor_tensor(prod[:, lo:hi], SUMS[part][:, 0:n * NE * HD].rearrange("p (h e d) -> p h e d", e=NE, d=HD),
                                  q.unsqueeze(2).to_broadcast([P, n, NE, HD]), ALU.mult).then_inc(l_read, 1)

            def quotient(t):
                dve.wait_ge(l_read, 3 * t + 3)
                link(dve.tensor_reduce(num[:], prod[:], AX.X, ALU.add))
                link(dve.tensor_scalar(den3[:].unsqueeze(2), num[:, :, HD:NE], EPS_LINEAR, None, ALU.add))
                link(dve.reciprocal(rec3[:], den3[:]))
                wait(dve, l_oT, t)
                dve.tensor_tensor(o3[:].rearrange("p (h d) -> p h d", d=HD), num[:, :, 0:HD],
                                  rec3[:].unsqueeze(2).to_broadcast([P, HEADS, HD]), ALU.mult).then_inc(l_o, 1)

            def residual3(t, k):
                dve.wait_ge(l_y, t + 1)
                wait(dve, x3_ready, t - 1)
                i = k % 2
                dve.tensor_tensor(z3[i][:], Y3[:, 0:P], bo[:], ALU.add).then_inc(l_yread, 1)
                dve.wait_ge(l_yread, t + 1)
                link(dve.tensor_tensor(z3[i][:], z3[i][:], tile_of(X, t), ALU.add))
                statistics(z3[i][:].unsqueeze(1), mvp[i], 1, l_stats)

            def batch3(n):
                for k in range(PER_BATCH):
                    t = PER_BATCH * n + k
                    attend(t, k, 0)
                    attend(t, k, 1)
                    if there(t + 2):
                        features(t + 2, k + 2)
                    attend(t, k, 2)
                    if there(t + 2):
                        elu(t + 2, k + 2)
                    quotient(t)
                    if there(t - 1):
                        residual3(t - 1, k - 1)

            dve.wait_ge(x2_ready, GROUPS)
            for i in range(4):
                link(dve.memset(va3[i][:], 1.0))
            for t in range(2):
                features(t, t)
                elu(t, t)
            batch3(0)
            LINKS = 4 * PER_BATCH
            with dve.Fori(1, BATCH - 1) as n:
                link.before(n - 1, LINKS)
                batch3(n)
            link.after(BATCH - 2, LINKS)
            batch3(BATCH - 1)
            residual3(TILES - 1, PER_BATCH - 1)

            U4, V4, Y4 = psum[0:2], psum[2:4], psum[7]

            def gate(g):
                for o in range(HC):
                    i = o % 2
                    dve.wait_ge(g_th, HC * g + o + 1)
                    link(dve.scalar_tensor_tensor(out=t4[i][:], in0=th4[i][:], scalar=1.0, in1=U4[i][:],
                                                  op0=ALU.add, op1=ALU.mult))
                    dve.wait_ge(g_v, HC * g + o + 1)
                    dve.tensor_tensor(ha[:, o, :], t4[i][:], V4[i][:], ALU.mult).then_inc(g_ha, 1)

            def residual4(g):
                dve.wait_ge(g_y, g + 1)
                wait(dve, x4_ready, g)
                dve.tensor_tensor(zt[0][:], Y4[:].rearrange("p (t n) -> p t n", t=GT),
                                  X[:, bass.ds(GT * g, GT), :], ALU.add).then_inc(g_z, 1)
                dve.wait_ge(g_z, g + 1)
                statistics(zt[0][:], mvp[0], GT, g_stats)

            gate(0)
            LINKS = HC
            with dve.Fori(1, GROUPS) as g:
                link.before(g - 1, LINKS)
                gate(g)
                residual4(g - 1)
            link.after(GROUPS - 1, LINKS)
            residual4(GROUPS - 1)

        @block.gpsimd
        def _(pool):
            link = Chain(pool, pool_own)
            pool.wait_ge(x_in, 16 * BATCH)
            pool.wait_ge(consts_ready, 2)

            def inverse_std(r, m, count):
                link(pool.tensor_tensor(r[:, 0:count].unsqueeze(2), m[:, 0:count, 1:2], eps[:, 0:count].unsqueeze(2), ALU.add))
                link(pool.tensor_tensor(r[:, 0:count], r[:, 0:count], half[:, 0:count], ALU.pow))

            def spread(col):
                return col.unsqueeze(2).to_broadcast([P, col.shape[1], P])

            def inner_norm(w):
                pool.wait_ge(y_stats, w + 1)
                inverse_std(rs, mv, 1)
                link(pool.tensor_tensor(z1[:], fused[:], mv[:, 0, 0:1].to_broadcast([P, P]), ALU.subtract))
                link(pool.tensor_tensor(z1[:], z1[:], rs[:, 0:1].to_broadcast([P, P]), ALU.mult))
                link(pool.tensor_tensor(z1[:], z1[:], gamma[:], ALU.mult))
                pool.tensor_tensor(z1[:], z1[:], beta[:], ALU.add)
                pool.drain()
                pool.tensor_tensor(z1[:], z1[:], tile_of(X, w), ALU.add).then_inc(z_ready, 1)

            def outer_norm(w):
                pool.wait_ge(z_stats, w + 1)
                inverse_std(rs2, mv2, 1)
                pool.tensor_tensor(z1[:], z1[:], mv2[:, 0, 0:1].to_broadcast([P, P]), ALU.subtract)
                pool.drain()
                pool.tensor_tensor(tile_of(X, w), z1[:], rs2[:, 0:1].to_broadcast([P, P]), ALU.mult).then_inc(x1_ready, 1)

            def split_values(u, b):
                pool.wait_ge(qkv_read, u + 1)
                one = ones.rearrange("p (h d) -> p h d", d=HD)
                v, part = v32[b][:], [vs[b][:, :, c * HD:(c + 1) * HD] for c in range(VP)]
                wait(pool, o_done, u - 1)
                link(pool.tensor_tensor(part[0], v, one, ALU.mult))
                link(pool.tensor_tensor(vr[:], v, part[0], ALU.subtract))
                link(pool.tensor_tensor(part[1], vr[:], one, ALU.mult))
                pool.tensor_tensor(part[2], vr[:], part[1], ALU.subtract).then_inc(v_ready, 1)
                pool.wait_ge(v_ready, u + 1)

            def low_part(u, b, g):
                pool.wait_ge(high_ready, G * u + g + 1)
                pool.tensor_tensor(prl[:, b, g, :], probs[:, b, g, :], prh[:, b, g, :], ALU.subtract).then_inc(lo_ready[0], 1)

            def steps(w):
                for b in range(2):
                    u = 2 * w + b
                    if there(u, UNITS):
                        low_part(u, b, 0)
                        low_part(u, b, 1)
                    if there(u + 1, UNITS):
                        split_values(u + 1, 1 - b)
                    if there(w - 2):
                        (inner_norm, outer_norm)[b](w - 2)

            LINKS = 7 + 2 * 3
            windows(pool, steps, link, LINKS)

            def norm(stats, ready, n, z, m, first_tile, count):
                pool.wait_ge(stats, n + 1)
                inverse_std(rs, m, count)
                pool.tensor_tensor(z, z, spread(m[:, 0:count, 0]), ALU.subtract)
                pool.drain()
                pool.tensor_tensor(X[:, bass.ds(first_tile, count), :], z, spread(rs[:, 0:count]), ALU.mult).then_inc(ready, 1)
                pool.wait_ge(ready, n + 1)

            with pool.Fori(0, BATCH) as n:
                link.before(n, 4)
                for h in range(2):
                    norm(f_stats, x2_ready, 2 * n + h, zt[h][:], mvp[h], (2 * n + h) * GT, GT)
            link.after(BATCH, 4)

            def products(t, k):
                pool.wait_ge(l_phi, t + 1)
                wait(pool, l_y, 1 if isinstance(t, int) and t == 2 else t - 2)
                pool.tensor_tensor(kv[k % 2][:], va3[k % 4][:].unsqueeze(3).to_broadcast([P, HEADS, NE, HD]),
                                   phi[k % 4][:, 1, :].rearrange("p (h d) -> p h d", d=HD).unsqueeze(2)
                                   .to_broadcast([P, HEADS, NE, HD]), ALU.mult).then_inc(l_kv, 1)

            def batch3(n):
                for k in range(PER_BATCH):
                    t = PER_BATCH * n + k
                    if there(t + 1):
                        products(t + 1, k + 1)
                    if there(t - 1):
                        i = (k - 1) % 2
                        norm(l_stats, x3_ready, t - 1, z3[i][:].unsqueeze(1), mvp[i], t - 1, 1)

            products(0, 0)
            batch3(0)
            LINKS = 2 * PER_BATCH
            with pool.Fori(1, BATCH - 1) as n:
                link.before(n - 1, LINKS)
                batch3(n)
            link.after(BATCH - 2, LINKS)
            batch3(BATCH - 1)
            norm(l_stats, x3_ready, TILES - 1, z3[1][:].unsqueeze(1), mvp[1], TILES - 1, 1)

            with pool.Fori(0, GROUPS) as g:
                link.before(g, 2)
                norm(g_stats, x4_ready, g, zt[0][:], mvp[0], GT * g, GT)
            link.after(GROUPS, 2)


def kernel(**inputs):
    from concourse import bacc
    from concourse.bass_utils import run_bass_kernel_spmd

    v = {n: np.asarray(x) for n, x in inputs.items()}
    L0, F0, L1, F1 = "L0_attn_", "L0_ffn_", "L1_attn_", "L1_ffn_"
    x = v[L0 + "x"].reshape(BATCH * SEQ, P)
    arrays = {
        "x": x, "xT": x.T, "cst": constants(),
        "projT0": v[L0 + "proj_local"].T, "projT1": v[L0 + "proj_global"].T,
        "fusion": v[L0 + "fusion_w"], "gamma": v[L0 + "ln_gamma"], "beta": v[L0 + "ln_beta"],
        "wrT": v[F0 + "W_r"].T, "wkT": v[F0 + "W_k"].T, "wvT": v[F0 + "W_v"].T,
        "mu": np.stack([v[F0 + "mu_r"], v[F0 + "mu_k"]], axis=1), "w3_s": v[F1 + "w3_s"],
        "scol": np.stack([v[F1 + n].reshape(HC, P).T for n in ("w1_s", "w2_s", "h1_s", "h2_s")], axis=1),
        "w1T": v[F1 + "w1_w"].T, "w2T": v[F1 + "w2_w"].T, "w3T": v[F1 + "w3_w"].T,
        "h1T": v[F1 + "h1_w"].T, "h2T": v[F1 + "h2_w"].T,
    }
    for b, n in enumerate("lg"):
        arrays[f"winT{b}"] = v[f"{L0}W{n}_in"].T
        arrays[f"bin{b}"] = v[f"{L0}b{n}_in"]
        arrays[f"bcol{b}"] = v[f"{L0}b{n}_in"].reshape(3, P).T
        arrays[f"woutT{b}"] = v[f"{L0}W{n}_out"].T
        arrays[f"bout{b}"] = v[f"{L0}b{n}_out"]
    for n in "qkvo":
        arrays[f"lw{n}T"] = v[f"{L1}W{n}"].T
        arrays[f"lb{n}"] = v[f"{L1}b{n}"]
    arrays = {n: np.ascontiguousarray(t) for n, t in arrays.items()}

    nc = bacc.Bacc("TRN2", target_bir_lowering=False, num_devices=1)
    dram = {n: nc.dram_tensor(f"in_{n}", t.shape, mybir.dt.from_np(t.dtype), kind="ExternalInput").ap()
            for n, t in arrays.items()}
    out = nc.dram_tensor("out_y", [BATCH * SEQ, P], F32, kind="ExternalOutput").ap()
    build(nc, dram, out)
    r = run_bass_kernel_spmd(nc, [{f"in_{n}": t for n, t in arrays.items()}], core_ids=[0])
    return r.results[0]["out_y"].reshape(BATCH, SEQ, P)
```

```python
from contextlib import ExitStack

import numpy as np

import concourse.bass as bass
from concourse import mybir

F32 = mybir.dt.float32
BF16 = mybir.dt.bfloat16
F16 = mybir.dt.float16
I32 = mybir.dt.int32
F32R = mybir.dt.float32r
ALU = mybir.AluOpType
ACT = mybir.ActivationFunctionType
AX = mybir.AxisListType

P = 128
BATCH, SEQ = 8, 1024
TILES = BATCH * SEQ // P
UNITS = 2 * TILES
PER_BATCH = SEQ // P
HEADS, HD = 16, 8
RING = 4
J = 4
G = HEADS // J
HIDDEN = 512
HC = HIDDEN // P
GT = 4
GROUPS = TILES // GT
NE = HD + 1
EPS = 1e-5
EPS_LINEAR = 1e-6
VP = 3
NV = VP * HD + 1
SHIFT = 4.875
SPLIT = [(0, 6), (6, 11), (11, 16)]

W4_UP, W4_H1 = 0, 2 * HIDDEN
W4_H2 = W4_H1 + HC * HIDDEN
W4_DOWN = W4_H2 + HC * HIDDEN
W4_END = W4_DOWN + HC * P
PIECE = W4_END // BATCH

C_ID, C_UT, C_LT, C_ONE, C_TRI = 0, P, 2 * P, 3 * P, 4 * P
C_MQ = C_TRI + P
C_MK = C_MQ + J
C_MM = C_MK + G
C_END = C_MM + HEADS


def constants():
    c = np.zeros((P, C_END), np.float32)
    p = np.arange(P)
    c[:, C_ID:C_ID + P] = np.eye(P)
    c[:, C_UT:C_UT + P] = p[:, None] <= p[None, :]
    c[:, C_LT:C_LT + P] = p[:, None] > p[None, :]
    c[:, C_ONE:C_ONE + P] = 1.0
    c[:, C_TRI:C_TRI + P] = SHIFT + (p[:, None] > p[None, :])
    for j in range(J):
        c[:, C_MQ + j] = (p // HD % J == j) * np.float32(1 / np.sqrt(np.float32(HD)))
        c[:, C_MK + j] = p // (J * HD) == j
        for g in range(G):
            c[[J * HD * g + j, J * HD * g + HD + j], C_MM + J * g + j] = 1.0
    return c


def wait(eng, sem, value):
    if not isinstance(value, int) or value > 0:
        eng.wait_ge(sem, value)


class Chain:

    def __init__(self, eng, sem):
        self.eng, self.sem, self.base, self.k, self.past = eng, sem, 0, 0, 0

    def __call__(self, ins):
        self.k += 1
        ins.then_inc(self.sem, 1)
        self.eng.wait_ge(self.sem, self.past + (self.base + self.k))

    def before(self, passed, links):
        self.base, self.k = self.base + self.k, 0
        self.past = passed * links

    def after(self, passes, links):
        assert self.k == links, (self.k, links)
        self.base, self.k, self.past = self.base + links * passes, 0, 0


def there(t, count=TILES):
    return not isinstance(t, int) or 0 <= t < count


def windows(eng, steps, chain=None, links=0):
    for w in (-1, 0, 1):
        steps(w, w % 2)
    with eng.Fori(1, TILES // 2 - 1) as n:
        if chain:
            chain.before(n - 1, links)
        steps(2 * n, 0)
        steps(2 * n + 1, 1)
    if chain:
        chain.after(TILES // 2 - 2, links)
    for w in range(TILES - 2, TILES + 2):
        steps(w, w % 2)


def tile_of(X, t):
    return X[:, bass.ds(t, 1), :].rearrange("p a n -> p (a n)")


def build(nc, a, out):
    with ExitStack() as ctx:
        def sb(name, shape, dt=F32):
            return ctx.enter_context(nc.sbuf_tensor(name, shape, dt))

        def sem(name):
            return ctx.enter_context(nc.semaphore(name))

        psum = [ctx.enter_context(nc.psum_tensor(f"bank{i}", [P, 512], F32)) for i in range(8)]

        X = sb("X", [P, TILES, P])
        cst = sb("cst", [P, C_END])
        ident = cst[:, C_ID:C_ID + P]
        upper = cst[:, C_UT:C_UT + P]
        lower = cst[:, C_LT:C_LT + P]
        ones = cst[:, C_ONE:C_ONE + P]
        ident_b = sb("ident_b", [P, P], BF16)
        tri_b = sb("tri_b", [P, J, P], BF16)
        pick_b = sb("pick_b", [P, HEADS, P], BF16)
        half = sb("half", [P, GT])
        eps = sb("eps", [P, GT])

        loads = []

        def load(name, shape, src):
            t = sb(name, shape)
            loads.append((t[:], src))
            return t

        loads.append((cst[:], a["cst"]))
        projT = [load(f"projT{b}", [P, P], a[f"projT{b}"]) for b in range(2)]
        winT = [load(f"winT{b}", [P, 3 * P], a[f"winT{b}"]) for b in range(2)]
        woutT = [load(f"woutT{b}", [P, P], a[f"woutT{b}"]) for b in range(2)]
        bq = [load(f"bq{b}", [P, 3], a[f"bcol{b}"]) for b in range(2)]
        bv = [load(f"bv{b}", [P, P], a[f"bin{b}"][2 * P:3 * P].partition_broadcast(P)) for b in range(2)]
        bout = [load(f"bout{b}", [P, P], a[f"bout{b}"].partition_broadcast(P)) for b in range(2)]
        fw = load("fw", [P, 2], a["fusion"].partition_broadcast(P))
        gamma = load("gamma", [P, P], a["gamma"].partition_broadcast(P))
        beta = load("beta", [P, P], a["beta"].partition_broadcast(P))
        first_loads, loads = loads, []
        wrT = load("wrT", [P, P], a["wrT"])
        wkT = load("wkT", [P, P], a["wkT"])
        wvT = load("wvT", [P, P], a["wvT"])
        mu = load("mu", [P, 2], a["mu"])
        wqkvT = sb("wqkvT", [P, 3, P])
        bqkvo = sb("bqkvo", [P, 4, P])
        for i, n in enumerate("qkv"):
            loads.append((wqkvT[:, i, :], a[f"lw{n}T"]))
            loads.append((bqkvo[:, i, :], a[f"lb{n}"].partition_broadcast(P)))
        woT = load("woT", [P, P], a["lwoT"])
        loads.append((bqkvo[:, 3, :], a["lbo"].partition_broadcast(P)))
        b3 = sb("b3", [P, 4, P], BF16)
        ones_b = sb("ones_b", [P, P], BF16)
        upper_r = sb("upper_r", [P, P], F32R)
        lower_r = sb("lower_r", [P, P], F32R)
        w4h = sb("w4h", [P, W4_END], F32R)
        w4l = sb("w4l", [P, W4_END], F32R)
        low_any = sb("low_any", [P, BATCH])
        low_sum = sb("low_sum", [P, 1])
        low_count = sb("low_count", [1, 1])
        scol = load("scol", [P, 4, HC], a["scol"])
        s3 = load("s3", [P, P], a["w3_s"].partition_broadcast(P))

        first_in, weights_in, x_in, consts_ready = sem("first_in"), sem("weights_in"), sem("x_in"), sem("consts_ready")
        setup_pe, setup_act, setup_dve = sem("setup_pe"), sem("setup_act"), sem("setup_dve")
        w4_in, w4_high, w4_ready = sem("w4_in"), sem("w4_high"), sem("w4_ready")
        low_counted, low_known = sem("low_counted"), sem("low_known")
        dve_own, pool_own, act_own = sem("dve_own"), sem("pool_own"), sem("act_own")
        stored = sem("stored")

        x_tok = a["x"].rearrange("(t p) n -> p t n", p=P)
        xT_win = a["xT"].rearrange("p (t n) -> p t n", n=P)
        out_tok = out.rearrange("(t p) n -> p t n", p=P)

        wcT = [sb(f"wcT{b}", [P, 3 * P]) for b in range(2)]
        wos = [sb(f"wos{b}", [P, P]) for b in range(2)]
        fbias = sb("fbias", [P, P])
        fsm = sb("fsm", [P, 8])
        omu = sb("omu", [P, 2])
        halfs = sb("halfs", [P, 2, HC])
        fb1 = sb("fb1", [P, P])
        bsplit = sb("bsplit", [P, 4, P], BF16)
        fsplit = sb("fsplit", [P, 2, 4, P])

        st6 = sb("st6", [P, GT, 6])
        rs = sb("rs", [P, GT])
        mvp = [sb(f"mvp{i}", [P, GT, 2]) for i in range(2)]
        xg = sb("xg", [P, GT * P])
        zt = [sb(f"zt{i}", [P, GT, P]) for i in range(2)]

        own_stage = ctx.enter_context(ExitStack())

        def st(name, shape, dt=F32):
            return own_stage.enter_context(nc.sbuf_tensor(name, shape, dt))

        xTw = st("xTw", [P, P])
        qx = [st(f"qx{i}", [P, J, P]) for i in range(RING)]
        kz = [st(f"kz{i}", [P, G, P]) for i in range(RING)]
        qxb = [st(f"qxb{i}", [P, J, P], F32R) for i in range(RING)]
        kzb = [st(f"kzb{i}", [P, G, P], F32R) for i in range(RING)]
        v32 = [st(f"v32{i}", [P, HEADS, HD]) for i in range(2)]
        vr = st("vr", [P, HEADS, HD])
        vs = [st(f"vs{i}", [P, HEADS, NV], BF16) for i in range(2)]
        m32 = [st(f"m32{i}", [P, J, G]) for i in range(2)]
        mx = [st(f"mx{i}", [P, P], BF16) for i in range(2)]
        mxT = [st(f"mxT{i}", [P, P], BF16) for i in range(2)]
        probs = st("probs", [P, 2, G, J * P])
        pr = [[probs[:, i, g, :].rearrange("p (j q) -> p j q", j=J) for g in range(G)] for i in range(2)]
        prh = st("prh", [P, 2, G, J * P], F16)
        prl = st("prl", [P, 2, G, J * P], F16)
        osum = [st(f"osum{i}", [P, HEADS, HD]) for i in range(2)]
        rec = [st(f"rec{i}", [P, HEADS]) for i in range(2)]
        on = [st(f"on{i}", [P, P]) for i in range(2)]
        onT = [st(f"onT{i}", [P, P]) for i in range(2)]
        fused = st("fused", [P, P])
        mv = st("mv", [P, GT, 2])
        mv2 = st("mv2", [P, GT, 2])
        rs2 = st("rs2", [P, GT])
        z1 = st("z1", [P, P])

        xT_in = sem("xT_in")
        qkv_done, qkv_read = sem("qkv_done"), sem("qkv_read")
        q_ready, k_ready, bf_ready = sem("q_ready"), sem("k_ready"), sem("bf_ready")
        v_ready, m_reduced, lo_ready = sem("v_ready"), sem("m_reduced"), [sem("lo_pool"), sem("lo_dve")]
        high_ready = sem("high_ready")
        mq_done, max_ready = sem("mq_done"), sem("max_ready")
        mT_done, mxT_ready = sem("mT_done"), sem("mxT_ready")
        s_done = sem("s_done")
        o_done, o_read, on_ready = sem("o_done"), sem("o_read"), sem("on_ready")
        oT_done, onT_ready = sem("oT_done"), sem("onT_ready")
        y_done, y_stats, y_read = sem("y_done"), sem("y_stats"), sem("y_read")
        z_ready, z_stats, x1_ready = sem("z_ready"), sem("z_stats"), sem("x1_ready")

        PJ, M, S, OB, TR, Y = psum[0], psum[1:3], psum[3:5], psum[5], psum[6], psum[7]

        own_stage.close()
        xs = [st(f"xs{h}", [P, 1 + GT * P]) for h in range(2)]
        xmix = [[st(f"xmix{h}{i}", [P, GT * P]) for i in range(2)] for h in range(2)]
        tmp = [st(f"tmp{i}", [P, GT * P]) for i in range(2)]
        ka = st("ka", [P, GT * P])
        th = st("th", [P, GT * P])
        w4 = st("w4", [P, W4_END])
        w4_loads = [(w4[:, W4_DOWN:W4_END].rearrange("p (c n) -> p c n", n=P), a["w3T"].rearrange("(c p) n -> p c n", p=P))]
        for n, at, rows in (("w1T", W4_UP, P), ("w2T", W4_UP + HIDDEN, P), ("h1T", W4_H1, HIDDEN), ("h2T", W4_H2, HIDDEN)):
            cols = slice(at, at + rows // P * HIDDEN)
            w4_loads.append((w4[:, cols].rearrange("p (c n) -> p c n", n=HIDDEN), a[n].rearrange("(c p) n -> p c n", p=P)))
        f_xg, f_tr, f_xs, f_mix, f_k, f_ka, f_r, f_th, f_v, f_z, f_stats, x2_ready = map(sem, (
            "f_xg", "f_tr", "f_xs", "f_mix", "f_k", "f_ka", "f_r", "f_th", "f_v", "f_z", "f_stats", "x2_ready"))

        own_stage.close()
        xg3 = [st(f"xg3{i}", [P, P]) for i in range(2)]
        xT3 = st("xT3", [P, P])
        relu3 = [st(f"relu3{i}", [P, 2, P]) for i in range(2)]
        ex3 = [st(f"ex3{i}", [P, 2, P]) for i in range(2)]
        va3 = [st(f"va3{i}", [P, HEADS, NE]) for i in range(2)]
        phi = [st(f"phi{i}", [P, 2, P]) for i in range(4)]
        kv = [st(f"kv{i}", [P, HEADS, NE, HD]) for i in range(2)]
        kvh = [st(f"kvh{i}", [P, HEADS, NE, HD], F32R) for i in range(2)]
        kvl = [st(f"kvl{i}", [P, HEADS, NE, HD], F32R) for i in range(2)]
        prod = st("prod", [P, HEADS, NE, HD])
        num = st("num", [P, HEADS, NE])
        rec3 = st("rec3", [P, HEADS])
        den3 = st("den3", [P, HEADS])
        o3 = st("o3", [P, P])
        oT3 = st("oT3", [P, P])
        z3 = [st(f"z3{i}", [P, P]) for i in range(2)]
        (l_xg, l_tr, l_xT, l_qkv, l_qread, l_phi, l_kv, l_kvh, l_kvl, l_kvl2, l_cum, l_ones, l_num, l_den, l_rec,
         l_read, l_yread, l_o, l_oT, l_oTs, l_y, l_stats, x3_ready) = map(sem, (
            "l_xg", "l_tr", "l_xT", "l_qkv", "l_qread", "l_phi", "l_kv", "l_kvh", "l_kvl", "l_kvl2", "l_cum", "l_ones",
            "l_num", "l_den", "l_rec",
            "l_read", "l_yread", "l_o", "l_oT", "l_oTs", "l_y", "l_stats", "x3_ready"))

        own_stage.close()
        xTh = st("xTh", [P, GT * P], F32R)
        xTl = st("xTl", [P, GT * P], F32R)
        th4 = [st(f"th4{i}", [P, GT * P]) for i in range(2)]
        t4 = [st(f"t4{i}", [P, GT * P]) for i in range(2)]
        gated = [st(f"gated{i}", [P, GT * P]) for i in range(2)]
        hid = [st(f"hid{i}", [P, GT * P]) for i in range(2)]
        (hah, hal, hbh, hbl, hch, hcl) = [st(n, [P, HC, GT * P], F32R) for n in ("hah", "hal", "hbh", "hbl", "hch", "hcl")]
        y4 = st("y4", [P, GT, P])
        (g_xg, g_tr, g_xTh, g_xT, g_u, g_th, g_v, g_gate, g_hah, g_ha, g_l1, g_act1, g_hb, g_l2, g_act2, g_hc, g_y, g_yread, g_z,
         g_stats, x4_ready) = map(sem, (
            "g_xg", "g_tr", "g_xTh", "g_xT", "g_u", "g_th", "g_v", "g_gate", "g_hah", "g_ha", "g_l1", "g_act1", "g_hb", "g_l2",
            "g_act2", "g_hc", "g_y", "g_yread", "g_z", "g_stats", "x4_ready"))

        block = ctx.enter_context(nc.Block())

        @block.sync
        def _(sp):
            for dst, src in first_loads[::2]:
                sp.dma_start(dst, src).then_inc(first_in, 16)
            sp.dma_start(xTw[:], xT_win[:, 0, :]).then_inc(xT_in, 16)
            for b in range(BATCH):
                ts = slice(b * PER_BATCH, (b + 1) * PER_BATCH)
                sp.dma_start(X[:, ts, :], x_tok[:, ts, :]).then_inc(x_in, 16)
            for dst, src in loads:
                sp.dma_start(dst, src).then_inc(weights_in, 16)

            with sp.Fori(1, TILES) as w:
                sp.wait_ge(qkv_done, 2 * w)
                sp.dma_start(xTw[:], xT_win[:, bass.ds(w, 1), :].rearrange("p a n -> p (a n)")).then_inc(xT_in, 16)

            sp.wait_ge(x1_ready, TILES)
            for dst, src in w4_loads:
                sp.dma_start(dst, src).then_inc(w4_in, 16)

            with sp.Fori(0, GROUPS) as g:
                sp.wait_ge(x4_ready, g + 1)
                sp.dma_start(out_tok[:, bass.ds(g * GT, GT), :], X[:, bass.ds(g * GT, GT), :]).then_inc(stored, 16)
            sp.wait_ge(stored, 16 * GROUPS)

        @block.tensor
        def _(pe):
            pe.wait_ge(first_in, 16 * len(first_loads))
            for b in range(2):
                pe.matmul(psum[b][:, 0:3 * P], projT[b][:], winT[b][:], start=True, stop=True).then_inc(setup_pe, 1)
            pe.wait_ge(consts_ready, 1)

            def project(u, b):
                if b == 0:
                    pe.wait_ge(xT_in, 8 * u + 16)
                wait(pe, qkv_read, u)
                pe.matmul(PJ[:, 0:P], wcT[b][:, 0:P], xTw[:], start=True, stop=True)
                pe.matmul(PJ[:, P:2 * P], wcT[b][:, P:2 * P], xTw[:], start=True, stop=True)
                pe.matmul(PJ[:, 2 * P:3 * P], xTw[:], wcT[b][:, 2 * P:3 * P], start=True, stop=True).then_inc(qkv_done, 1)

            def max_scores(u, r, j):
                if j == 0:
                    pe.wait_ge(bf_ready, 2 * u + 2)
                wait(pe, m_reduced, J * u + j - 1)
                pe.matmul(M[j % 2][:], qxb[r][:, j, :], kzb[r][:].rearrange("p g k -> p (g k)"),
                          start=True, stop=True).then_inc(mq_done, 1)

            def turn_max(u, b):
                pe.wait_ge(max_ready, u + 1)
                wait(pe, onT_ready, u - 2)
                pe.transpose(TR[:].bitcast(BF16)[:, 0:P], mx[b][:], ident_b[:]).then_inc(mT_done, 1)

            def scores(u, b, r, g):
                if g == 0:
                    if isinstance(u, int) and u == 0:
                        pe.wait_ge(consts_ready, 2)
                    pe.wait_ge(mxT_ready, u + 1)
                wait(pe, high_ready, G * u + g - 1)
                s = S[g % 2][:]
                pe.matmul(s, kz[r][:, g, :], qx[r][:].rearrange("p j q -> p (j q)"), start=True, stop=False)
                for j in range(J):
                    pe.matmul(s[:, j * P:(j + 1) * P], pick_b[:, J * g + j, :], mxT[b][:], start=False, stop=False)
                pe.matmul(s, ident_b[:], tri_b[:].rearrange("p j q -> p (j q)"), start=False, stop=True).then_inc(s_done, 1)

            def values(u, b, g):
                if g == 0:
                    wait(pe, o_read, u)
                    pe.wait_ge(v_ready, u + 1)
                pe.wait_ge(high_ready, G * u + g + 1)
                pe.wait_ge(lo_ready[g // 2], 2 * u + g % 2 + 1)
                for j in range(J):
                    h = G * g + j
                    cols = slice(j * P, (j + 1) * P)
                    pe.matmul(OB[:, h * NV:(h + 1) * NV], prh[:, b, g, cols], vs[b][:, h, :], start=True, stop=False)
                    mm = pe.matmul(OB[:, h * NV:(h + 1) * NV], prl[:, b, g, cols], vs[b][:, h, :], start=False, stop=True)
                if g == G - 1:
                    mm.then_inc(o_done, 1)

            def turn_out(u, b):
                pe.wait_ge(on_ready, u + 1)
                pe.wait_ge(mxT_ready, u + 3 if there(u + 2, UNITS) else UNITS)
                wait(pe, onT_ready, u)
                pe.transpose(TR[:, 0:P], on[b][:], ident).then_inc(oT_done, 1)

            def out_project(w):
                pe.wait_ge(onT_ready, 2 * w + 2)
                wait(pe, y_read, w)
                pe.matmul(Y[:, 0:P], onT[0][:], wos[0][:], start=True, stop=False)
                pe.matmul(Y[:, 0:P], onT[1][:], wos[1][:], start=False, stop=True).then_inc(y_done, 1)

            def steps(w, i):
                for b in range(2):
                    u, r = 2 * w + b, 2 * i + b
                    here, next_one, before = there(u, UNITS), there(u + 1, UNITS), there(u - 1, UNITS)
                    if here:
                        scores(u, b, r, 0)
                    if next_one:
                        max_scores(u + 1, (r + 1) % RING, 0)
                        max_scores(u + 1, (r + 1) % RING, 1)
                    if there(u - 2, UNITS):
                        turn_out(u - 2, b)
                    if here:
                        scores(u, b, r, 1)
                    if b == 1 and there(w - 1):
                        out_project(w - 1)
                    if next_one:
                        max_scores(u + 1, (r + 1) % RING, 2)
                    if before:
                        values(u - 1, 1 - b, 2)
                    if next_one:
                        max_scores(u + 1, (r + 1) % RING, 3)
                    if there(u + 2, UNITS):
                        project(u + 2, b)
                    if before:
                        values(u - 1, 1 - b, 3)
                    if here:
                        scores(u, b, r, 2)
                    if next_one:
                        turn_max(u + 1, 1 - b)
                    if here:
                        scores(u, b, r, 3)
                        values(u, b, 0)
                        values(u, b, 1)

            windows(pe, steps)

            K2, R2, V2, T2 = psum[0:4]
            pe.wait_ge(weights_in, 16 * len(loads))
            pe.wait_ge(x1_ready, TILES)

            def turn_x2(g):
                pe.wait_ge(f_xg, g + 1)
                wait(pe, f_xs, g)
                for t in range(GT):
                    mm = pe.transpose(T2[:, t * P:(t + 1) * P], xg[:, t * P:(t + 1) * P], ident)
                mm.then_inc(f_tr, 1)

            def shift_ffn(g, h, ahead=True):
                pe.wait_ge(f_mix, g + 1)
                wait(pe, f_ka, g)
                pe.matmul(K2[:], wkT[:], xmix[h][1][:], start=True, stop=True).then_inc(f_k, 1)
                wait(pe, f_th, g)
                for t in range(GT):
                    mm = pe.matmul(R2[:, t * P:(t + 1) * P], xmix[h][0][:, t * P:(t + 1) * P], wrT[:], start=True, stop=True)
                mm.then_inc(f_r, 1)
                if ahead:
                    turn_x2(g + 2)
                pe.wait_ge(f_ka, g + 1)
                wait(pe, f_z, g)
                for t in range(GT):
                    mm = pe.matmul(V2[:, t * P:(t + 1) * P], ka[:, t * P:(t + 1) * P], wvT[:], start=True, stop=True)
                mm.then_inc(f_v, 1)

            turn_x2(0)
            turn_x2(1)
            with pe.Fori(0, BATCH - 1) as n:
                shift_ffn(2 * n, 0)
                shift_ffn(2 * n + 1, 1)
            shift_ffn(GROUPS - 2, 0, ahead=False)
            shift_ffn(GROUPS - 1, 1, ahead=False)

            pe.wait_ge(w4_ready, BATCH + 1)
            pe.matmul(psum[7][:, 0:1], ones, low_sum[:], start=True, stop=True).then_inc(low_counted, 1)

            XT, QKV, SUMS, OT, Y3 = psum[0], psum[1], psum[2:5], psum[5], psum[6]
            pe.wait_ge(x2_ready, GROUPS)

            def turn_x3(t, k):
                pe.wait_ge(l_xg, t + 1)
                wait(pe, l_xT, t)
                pe.transpose(XT[:, 0:P], xg3[k % 2][:], ident).then_inc(l_tr, 1)

            def project3(t):
                pe.wait_ge(l_xT, t + 1)
                wait(pe, l_qread, t)
                pe.matmul(QKV[:, 0:3 * P], ones_b[:], b3[:, 0:3, :].rearrange("p c n -> p (c n)"), start=True, stop=False)
                pe.matmul(QKV[:, 0:3 * P], xT3[:], wqkvT[:].rearrange("p c n -> p (c n)"),
                          start=False, stop=True).then_inc(l_qkv, 1)

            def sums(k, part, matrix, start):
                lo, hi = SPLIT[part]
                for kvx in (kvh, kvl):
                    mm = pe.matmul(SUMS[part][:, 0:(hi - lo) * NE * HD], matrix[:],
                                   kvx[k % 2][:, lo:hi].rearrange("p h e d -> p (h e d)"),
                                   start=start and kvx is kvh, stop=True, skip_group_check=True)
                return mm

            def upto(t, k, part):
                if part != 1:
                    pe.wait_ge((l_kvl, None, l_kvl2)[part], t + 1)
                wait(pe, l_read, 3 * (t - 1) + part + 1)
                sums(k, part, upper_r, start=k == 0).then_inc(l_cum, 1)

            def behind(t, k, part):
                pe.wait_ge(l_read, 3 * t + part + 1)
                sums(k, part, lower_r, start=False)

            def turn_o3(t):
                pe.wait_ge(l_o, t + 1)
                wait(pe, l_oTs, t)
                pe.transpose(OT[:, 0:P], o3[:], ident).then_inc(l_oT, 1)

            def out_project3(t):
                pe.wait_ge(l_oTs, t + 1)
                wait(pe, l_yread, t)
                pe.matmul(Y3[:, 0:P], ones_b[:], b3[:, 3, :], start=True, stop=False)
                pe.matmul(Y3[:, 0:P], oT3[:], woT[:], start=False, stop=True).then_inc(l_y, 1)

            def batch3(n):
                for k in range(PER_BATCH):
                    t = PER_BATCH * n + k
                    for part in range(3):
                        upto(t, k, part)
                    if there(t + 2):
                        project3(t + 2)
                    if there(t + 3):
                        turn_x3(t + 3, k + 1)
                    if there(t - 1):
                        turn_o3(t - 1)
                    if k < PER_BATCH - 1:
                        for part in range(3):
                            behind(t, k, part)
                    if there(t - 1):
                        out_project3(t - 1)

            for t in range(2):
                turn_x3(t, t)
                project3(t)
            turn_x3(2, 0)
            batch3(0)
            with pe.Fori(1, BATCH - 1) as n:
                batch3(n)
            batch3(BATCH - 1)
            turn_o3(TILES - 1)
            out_project3(TILES - 1)

            U4, V4, L4, T4, Y4 = psum[0:2], psum[2:4], psum[4:6], psum[6], psum[7]
            pe.wait_ge(x3_ready, TILES)

            pe.wait_ge(low_known, 1)

            def products(bank, pairs, parts, turned=False, ready=None):
                for c, (w, x) in enumerate(pairs):
                    if ready:
                        pe.wait_ge(ready[0], ready[1] + (c + 1))
                    for n, (i, j) in enumerate(parts):
                        ab = (x[j], w[i]) if turned else (w[i], x[j])
                        mm = pe.matmul(bank, *ab, start=c == 0 and n == 0, stop=c == len(pairs) - 1 and n == len(parts) - 1)
                return mm

            def turn_x4(g):
                pe.wait_ge(g_xg, g + 1)
                wait(pe, g_xT, g)
                for t in range(GT):
                    mm = pe.transpose(T4[:, t * P:(t + 1) * P], xg[:, t * P:(t + 1) * P], ident)
                mm.then_inc(g_tr, 1)

            def up(g, o, parts):
                if o == 0:
                    pe.wait_ge(g_xT, g + 1)
                wait(pe, g_gate, HC * g + o - 1)
                for at, bank, done in ((W4_UP, U4, g_u), (W4_UP + HIDDEN, V4, g_v)):
                    cols = slice(at + o * P, at + (o + 1) * P)
                    products(bank[o % 2][:], [((w4h[:, cols], w4l[:, cols]), (xTh[:], xTl[:]))], parts).then_inc(done, 1)

            def hidden(g, o, parts, at, high, low, ready, done, read, read_before):
                if o >= 2:
                    pe.wait_ge(read, HC * g + o - 1)
                else:
                    wait(pe, read_before, HC * (g - (done is g_l1)) + o + 3)
                pairs = []
                for c in range(HC):
                    cols = slice(at + c * HIDDEN + o * P, at + c * HIDDEN + (o + 1) * P)
                    pairs.append(((w4h[:, cols], w4l[:, cols]), (high[:, c, :], low[:, c, :])))
                products(L4[o % 2][:], pairs, parts, ready=(ready, HC * g) if o == 0 else None).then_inc(done, 1)

            def down(g, parts):
                pe.wait_ge(g_hc, HC * g + HC)
                wait(pe, g_yread, g)
                for t in range(GT):
                    ts, pairs = slice(t * P, (t + 1) * P), []
                    for c in range(HC):
                        cols = slice(W4_DOWN + c * P, W4_DOWN + (c + 1) * P)
                        pairs.append(((w4h[:, cols], w4l[:, cols]), (hch[:, c, ts], hcl[:, c, ts])))
                    mm = products(Y4[:, ts], pairs, parts, turned=True)
                mm.then_inc(g_y, 1)

            def steps(g, parts):
                ahead = there(g + 1, GROUPS)
                for o in range(HC):
                    hidden(g, o, parts, W4_H1, hah, hal, g_ha, g_l1, g_act1, g_act2)
                    if ahead and o in (1, 2):
                        up(g + 1, o - 1, parts)
                if there(g - 1, GROUPS):
                    down(g - 1, parts)
                for o in range(HC):
                    hidden(g, o, parts, W4_H2, hbh, hbl, g_hb, g_l2, g_act2, g_act1)
                    if ahead and o < 2:
                        up(g + 1, o + 2, parts)
                    if o == 2 and there(g + 2, GROUPS):
                        turn_x4(g + 2)

            def groups(parts):
                turn_x4(0)
                for o in range(HC):
                    up(0, o, parts)
                turn_x4(1)
                steps(0, parts)
                with pe.Fori(1, GROUPS - 2) as g:
                    steps(g, parts)
                steps(GROUPS - 2, parts)
                steps(GROUPS - 1, parts)
                down(GROUPS - 1, parts)

            with pe.If(pe.value_load(low_count[:].bitcast(I32)) != 0):
                groups([(0, 0), (0, 1), (1, 0)])
            with pe.Else():
                groups([(0, 0), (0, 1)])

        @block.scalar
        def _(act):
            for dst, src in first_loads[1::2]:
                act.dma_start(dst, src).then_inc(first_in, 16)

            act.wait_ge(setup_dve, 1)
            act.activation(fsm[:, 4:6], fsm[:, 2:4], ACT.Exp).then_inc(setup_act, 1)

            def exp_scores(u, b, g):
                act.wait_ge(s_done, G * u + g + 1)
                act.activation(probs[:, b, g, :], S[g % 2][:], ACT.Exp)
                act.activation(prh[:, b, g, :], S[g % 2][:], ACT.Exp).then_inc(high_ready, 1)

            def read_out(u, b):
                act.wait_ge(oT_done, u + 1)
                act.activation(onT[b][:], TR[:, 0:P], ACT.Copy).then_inc(onT_ready, 1)

            def round_qk(u, r):
                act.wait_ge(q_ready, u + 1)
                act.activation(qxb[r][:], qx[r][:], ACT.Copy).then_inc(bf_ready, 1)
                act.wait_ge(k_ready, u + 1)
                act.activation(kzb[r][:], kz[r][:], ACT.Copy).then_inc(bf_ready, 1)

            def steps(w, i):
                for b in range(2):
                    u, r = 2 * w + b, 2 * i + b
                    if there(u, UNITS):
                        exp_scores(u, b, 0)
                    if there(u - 2, UNITS):
                        read_out(u - 2, b)
                    if there(u, UNITS):
                        exp_scores(u, b, 1)
                        exp_scores(u, b, 2)
                    if there(u + 2, UNITS):
                        round_qk(u + 2, (r + 2) % RING)
                    if there(u, UNITS):
                        exp_scores(u, b, 3)

            windows(act, steps)

            K2, R2, T2 = psum[0], psum[1], psum[3]
            own = Chain(act, act_own)
            act.wait_ge(x1_ready, TILES)

            def stage_x(g, turned, ready):
                wait(act, turned, g)
                act.activation(xg[:].rearrange("p (t n) -> p t n", t=GT), X[:, bass.ds(GT * g, GT), :], ACT.Copy).then_inc(ready, 1)

            def read_xT2(g, h):
                act.wait_ge(f_tr, g + 1)
                wait(act, f_mix, g - 1)
                if h:
                    act.activation(xs[1][:, 0:1], xs[0][:, GT * P:GT * P + 1], ACT.Copy)
                act.activation(xs[h][:, 1:1 + GT * P], T2[:], ACT.Copy).then_inc(f_xs, 1)

            def group2(g, h):
                act.wait_ge(f_k, g + 1)
                wait(act, f_v, g)
                own(act.activation(ka[:], K2[:], ACT.Relu))
                act.activation(ka[:], ka[:], ACT.Square).then_inc(f_ka, 1)
                if there(g + 2, GROUPS):
                    read_xT2(g + 2, h)
                if there(g + 3, GROUPS):
                    stage_x(g + 3, f_tr, f_xg)
                act.wait_ge(f_r, g + 1)
                wait(act, f_z, g)
                act.activation(th[:], R2[:], ACT.Tanh, scale=0.5).then_inc(f_th, 1)

            def split_w4(c):
                cols = bass.ds(c * PIECE, PIECE)
                act.activation(w4h[:, cols], w4[:, cols], ACT.Copy).then_inc(w4_high, 1)

            stage_x(0, f_tr, f_xg)
            read_xT2(0, 0)
            stage_x(1, f_tr, f_xg)
            read_xT2(1, 1)
            stage_x(2, f_tr, f_xg)
            group2(0, 0)
            group2(1, 1)
            act.wait_ge(w4_in, 16 * len(w4_loads))
            with act.Fori(1, BATCH - 2) as n:
                own.before(n - 1, 2)
                group2(2 * n, 0)
                split_w4(n - 1)
                group2(2 * n + 1, 1)
            own.after(BATCH - 3, 2)
            for n in (BATCH - 2, BATCH - 1):
                group2(2 * n, 0)
                split_w4(n - 1)
                if n == BATCH - 1:
                    split_w4(n)
                group2(2 * n + 1, 1)

            XT, QKV, OT = psum[0], psum[1], psum[5]
            act.wait_ge(x2_ready, GROUPS)
            act.wait_ge(low_known, 1)

            def stage_x3(t, k):
                wait(act, l_tr, t - 1)
                act.activation(xg3[k % 2][:], tile_of(X, t), ACT.Copy).then_inc(l_xg, 1)

            def read_x3(t):
                act.wait_ge(l_tr, t + 1)
                wait(act, l_qkv, t)
                act.activation(xT3[:], XT[:, 0:P], ACT.Copy).then_inc(l_xT, 1)

            def features(t, k):
                act.wait_ge(l_qkv, t + 1)
                wait(act, l_phi, t - 1)
                wait(act, l_kv, t - 1)
                qk = QKV[:, 0:2 * P].rearrange("p (c n) -> p c n", c=2)
                act.activation(relu3[k % 2][:], qk, ACT.Relu)
                act.activation(ex3[k % 2][:], qk, ACT.Exp)
                act.activation(va3[k % 2][:, :, 0:HD], QKV[:, 2 * P:3 * P].rearrange("p (h d) -> p h d", d=HD),
                               ACT.Copy).then_inc(l_qread, 1)

            def round_kv(t, k):
                act.wait_ge(l_kv, t + 1)
                wait(act, l_cum, 3 * (t - 1) + 1)
                act.activation(kvh[k % 2][:], kv[k % 2][:], ACT.Copy).then_inc(l_kvh, 1)

            def read_o3(t):
                act.wait_ge(l_oT, t + 1)
                wait(act, l_y, t)
                act.activation(oT3[:], OT[:, 0:P], ACT.Copy).then_inc(l_oTs, 1)

            def batch3(n):
                for k in range(PER_BATCH):
                    t = PER_BATCH * n + k
                    if there(t + 1):
                        round_kv(t + 1, k + 1)
                    if there(t + 2):
                        features(t + 2, k + 2)
                    if there(t - 1):
                        read_o3(t - 1)
                    if there(t + 3):
                        read_x3(t + 3)
                    if there(t + 4):
                        stage_x3(t + 4, k)

            stage_x3(0, 0)
            stage_x3(1, 1)
            act.wait_ge(l_ones, 1)
            read_x3(0)
            stage_x3(2, 0)
            features(0, 0)
            read_x3(1)
            stage_x3(3, 1)
            features(1, 1)
            read_x3(2)
            round_kv(0, 0)
            batch3(0)
            with act.Fori(1, BATCH - 1) as n:
                batch3(n)
            batch3(BATCH - 1)
            read_o3(TILES - 1)

            U4, L4, T4 = psum[0:2], psum[4:6], psum[6]
            act.wait_ge(x3_ready, TILES)

            def read_x4(g):
                act.wait_ge(g_tr, g + 1)
                act.activation(xTh[:], T4[:], ACT.Copy).then_inc(g_xTh, 1)

            def gate_tanh(g, o):
                act.wait_ge(g_u, HC * g + o + 1)
                wait(act, g_gate, HC * g + o - 1)
                act.activation(th4[o % 2][:], U4[o % 2][:], ACT.Tanh, scale=halfs[:, 0, o:o + 1]).then_inc(g_th, 1)

            def round_gated(g, o):
                act.wait_ge(g_gate, HC * g + o + 1)
                act.activation(hah[:, o, :], gated[o % 2][:], ACT.Copy).then_inc(g_hah, 1)

            def gelu(g, o, high, i, done, split, ready):
                act.wait_ge(done, HC * g + o + 1)
                wait(act, split, HC * g + o - 1)
                if o < 2:
                    wait(act, g_hc if split is g_hb else g_hb, HC * (g - (split is g_hb)) + o + 3)
                scale = scol[:, i, o:o + 1]
                act.activation(hid[o % 2][:], L4[o % 2][:], ACT.Gelu, scale=scale)
                act.activation(high[:, o, :], L4[o % 2][:], ACT.Gelu, scale=scale).then_inc(ready, 1)

            def steps(g):
                ahead = there(g + 1, GROUPS)
                for o in range(HC):
                    gelu(g, o, hbh, 2, g_l1, g_hb, g_act1)
                    if ahead and o in (1, 2):
                        gate_tanh(g + 1, o - 1)
                if ahead:
                    round_gated(g + 1, 0)
                    round_gated(g + 1, 1)
                for o in range(HC):
                    gelu(g, o, hch, 3, g_l2, g_hc, g_act2)
                    if ahead and o < 2:
                        gate_tanh(g + 1, o + 2)
                    if ahead and o in (1, 2):
                        round_gated(g + 1, o + 1)
                if there(g + 2, GROUPS):
                    read_x4(g + 2)
                if there(g + 3, GROUPS):
                    stage_x(g + 3, g_tr, g_xg)

            stage_x(0, g_tr, g_xg)
            read_x4(0)
            stage_x(1, g_tr, g_xg)
            gate_tanh(0, 0)
            gate_tanh(0, 1)
            round_gated(0, 0)
            gate_tanh(0, 2)
            round_gated(0, 1)
            gate_tanh(0, 3)
            round_gated(0, 2)
            round_gated(0, 3)
            read_x4(1)
            stage_x(2, g_tr, g_xg)
            steps(0)
            with act.Fori(1, GROUPS - 3) as g:
                steps(g)
            for g in range(GROUPS - 3, GROUPS):
                steps(g)

        @block.vector
        def _(dve):
            link = Chain(dve, dve_own)
            dve.memset(half[:], -0.5)
            dve.memset(eps[:], EPS)
            for i in range(2):
                dve.memset(vs[i][:], 1.0)
                dve.memset(mx[i][:], 0.0)
            dve.memset(ones_b[:], 1.0)
            dve.memset(b3[:], 0.0)
            dve.wait_ge(first_in, 16 * len(first_loads))
            link(dve.tensor_reduce(fsm[:, 0:1], fw[:], AX.X, ALU.max))
            dve.tensor_scalar(fsm[:, 2:4], fw[:], fsm[:, 0:1], None, ALU.subtract).then_inc(setup_dve, 1)
            dve.tensor_copy(ident_b[:], ident)
            dve.tensor_copy(tri_b[:], cst[:, C_TRI:C_TRI + P].unsqueeze(1).to_broadcast([P, J, P]))
            dve.wait_ge(setup_pe, 2)
            dve.tensor_copy(wcT[0][:], psum[0][:, 0:3 * P])
            dve.tensor_copy(wcT[1][:], psum[1][:, 0:3 * P]).then_inc(consts_ready, 1)
            dve.tensor_copy(pick_b[:], cst[:, C_MM:C_END].unsqueeze(2).to_broadcast([P, HEADS, P]))
            dve.wait_ge(setup_act, 1)
            link(dve.tensor_reduce(fsm[:, 6:7], fsm[:, 4:6], AX.X, ALU.add))
            link(dve.reciprocal(fsm[:, 7:8], fsm[:, 6:7]))
            link(dve.tensor_scalar(fsm[:, 0:2], fsm[:, 4:6], fsm[:, 7:8], None, ALU.mult))
            for b in range(2):
                dve.tensor_scalar(wos[b][:], woutT[b][:], fsm[:, b:b + 1], None, ALU.mult)
            link(dve.tensor_scalar(fb1[:], bout[0][:], fsm[:, 0:1], None, ALU.mult))
            dve.scalar_tensor_tensor(out=fbias[:], in0=bout[1][:], scalar=fsm[:, 1:2], in1=fb1[:],
                                     op0=ALU.mult, op1=ALU.add).then_inc(consts_ready, 1)
            dve.wait_ge(consts_ready, 2)

            def over(mask, n):
                return cst[:, mask:mask + n].unsqueeze(2).to_broadcast([P, n, P])

            def copies(bank, n):
                return bank.unsqueeze(1).to_broadcast([P, n, P])

            def read_qkv(u, b, r):
                dve.wait_ge(qkv_done, u + 1)
                wait(dve, v_ready, u - 1)
                dve.scalar_tensor_tensor(out=qx[r][:], in0=copies(PJ[:, 0:P], J), scalar=bq[b][:, 0:1],
                                         in1=over(C_MQ, J), op0=ALU.add, op1=ALU.mult).then_inc(q_ready, 1)
                dve.scalar_tensor_tensor(out=kz[r][:], in0=copies(PJ[:, P:2 * P], G), scalar=bq[b][:, 1:2],
                                         in1=over(C_MK, G), op0=ALU.add, op1=ALU.mult).then_inc(k_ready, 1)
                dve.tensor_tensor(v32[b][:], PJ[:, 2 * P:3 * P].rearrange("p (h d) -> p h d", d=HD),
                                  bv[b][:].rearrange("p (h d) -> p h d", d=HD), ALU.add).then_inc(qkv_read, 1)

            def reduce_max(u, b, j):
                dve.wait_ge(mq_done, J * u + j + 1)
                dve.tensor_reduce(m32[b][:, j, :], M[j % 2][:].rearrange("p (g k) -> p g k", g=G),
                                  AX.X, ALU.max, negate=True).then_inc(m_reduced, 1)

            def split_max(u, b):
                dve.wait_ge(m_reduced, J * u + J)
                m = m32[b][:].rearrange("p j g -> p g j")
                parts = mx[b][:].rearrange("p (g r) -> p g r", g=G)
                link(dve.tensor_copy(parts[:, :, 0:J], m))
                dve.tensor_tensor(parts[:, :, HD:HD + J], m, parts[:, :, 0:J], ALU.subtract).then_inc(max_ready, 1)

            def low_part(u, b, g):
                dve.wait_ge(high_ready, G * u + g + 1)
                dve.tensor_tensor(prl[:, b, g, :], probs[:, b, g, :], prh[:, b, g, :], ALU.subtract).then_inc(lo_ready[1], 1)

            def read_max(u, b):
                dve.wait_ge(mT_done, u + 1)
                dve.tensor_copy(mxT[b][:], TR[:].bitcast(BF16)[:, 0:P]).then_inc(mxT_ready, 1)

            def normalise(u, b):
                dve.wait_ge(o_done, u + 1)
                o = OB[:, 0:HEADS * NV].rearrange("p (h e) -> p h e", e=NV)
                dve.reciprocal(rec[b][:].unsqueeze(2), o[:, :, NV - 1:NV])
                dve.tensor_reduce(osum[b][:], o[:, :, 0:VP * HD].rearrange("p h (c d) -> p h d c", c=VP),
                                  AX.X, ALU.add).then_inc(o_read, 1)
                dve.wait_ge(o_read, u + 1)
                dve.tensor_tensor(on[b][:].rearrange("p (h d) -> p h d", d=HD), osum[b][:],
                                  rec[b][:].unsqueeze(2).to_broadcast([P, HEADS, HD]), ALU.mult).then_inc(on_ready, 1)

            def fuse(w):
                dve.wait_ge(y_done, w + 1)
                wait(dve, z_ready, w)
                dve.tensor_tensor(fused[:], Y[:, 0:P], fbias[:], ALU.add).then_inc(y_read, 1)
                dve.wait_ge(y_read, w + 1)
                dve.bn_stats(st6[:, 0, :], fused[:])
                dve.drain()
                dve.bn_aggr(mv[:, 0, :], st6[:, 0, :]).then_inc(y_stats, 1)

            def residual_stats(w):
                dve.wait_ge(z_ready, w + 1)
                dve.bn_stats(st6[:, 1, :], z1[:])
                dve.drain()
                dve.bn_aggr(mv2[:, 0, :], st6[:, 1, :]).then_inc(z_stats, 1)

            def steps(w, i):
                for b in range(2):
                    u, r = 2 * w + b, 2 * i + b
                    here, next_one, before = there(u, UNITS), there(u + 1, UNITS), there(u - 1, UNITS)
                    if next_one:
                        reduce_max(u + 1, 1 - b, 0)
                        reduce_max(u + 1, 1 - b, 1)
                    if before:
                        low_part(u - 1, 1 - b, 3)
                    if b == 1 and there(w - 2):
                        residual_stats(w - 2)
                    if next_one:
                        reduce_max(u + 1, 1 - b, 2)
                        reduce_max(u + 1, 1 - b, 3)
                        split_max(u + 1, 1 - b)
                    if before:
                        normalise(u - 1, 1 - b)
                    if next_one:
                        read_max(u + 1, 1 - b)
                    if there(u + 2, UNITS):
                        read_qkv(u + 2, b, (r + 2) % RING)
                    if b == 1 and there(w - 1):
                        fuse(w - 1)
                    if here:
                        low_part(u, b, 2)

            LINKS = 4
            windows(dve, steps, link, LINKS)

            V2 = psum[2]

            def statistics(z, m, count, done):
                for t in range(count):
                    dve.bn_stats(st6[:, t, :], z[:, t, :])
                dve.drain()
                for t in range(count):
                    last = dve.bn_aggr(m[:, t, :], st6[:, t, :])
                last.then_inc(done, 1)

            def mix(g, h):
                dve.wait_ge(f_xs, g + 1)
                wait(dve, f_r, g - 1)
                wait(dve, f_mix, g)
                for i in range(2):
                    last = dve.tensor_scalar(tmp[i][:], xs[h][:, 0:GT * P], omu[:, i:i + 1], None, ALU.mult)
                link(last)
                for i in range(2):
                    last = dve.scalar_tensor_tensor(out=xmix[h][i][:], in0=xs[h][:, 1:1 + GT * P], scalar=mu[:, i:i + 1],
                                                    in1=tmp[i][:], op0=ALU.mult, op1=ALU.add)
                last.then_inc(f_mix, 1)

            def low_w4(c):
                cols = bass.ds(c * PIECE, PIECE)
                dve.wait_ge(w4_high, c + 1)
                link(dve.tensor_tensor(w4l[:, cols], w4[:, cols], w4h[:, cols].bitcast(F32), ALU.subtract))
                link(dve.tensor_scalar(w4[:, cols], w4l[:, cols].bitcast(F32), 0.0, None, ALU.not_equal))
                dve.tensor_reduce(low_any[:, bass.ds(c, 1)], w4[:, cols], AX.X, ALU.max).then_inc(w4_ready, 1)

            def group2(g, h, ahead=True, pieces=()):
                if ahead:
                    mix(g + 1, 1 - h)
                for c in pieces:
                    low_w4(c)
                dve.wait_ge(f_v, g + 1)
                dve.wait_ge(f_th, g + 1)
                wait(dve, x2_ready, g - 1)
                z = zt[h][:]
                dve.scalar_tensor_tensor(out=z.rearrange("p t n -> p (t n)"), in0=th[:], scalar=1.0, in1=V2[:],
                                         op0=ALU.add, op1=ALU.mult).then_inc(f_z, 1)
                dve.wait_ge(f_z, g + 1)
                link(dve.scalar_tensor_tensor(out=z, in0=z, scalar=0.5, in1=X[:, bass.ds(GT * g, GT), :],
                                              op0=ALU.mult, op1=ALU.add))
                statistics(z, mvp[h], GT, f_stats)

            dve.wait_ge(x1_ready, TILES)
            dve.memset(xs[0][:, 0:1], 0.0)
            dve.wait_ge(weights_in, 16 * len(loads))
            link(dve.tensor_scalar(omu[:], mu[:], -1.0, 1.0, ALU.mult, ALU.add))
            dve.tensor_scalar(halfs[:, 0, :], scol[:, 0, :], 0.5, None, ALU.mult)
            link(dve.tensor_tensor(halfs[:, 1, :], scol[:, 0, :], scol[:, 1, :], ALU.mult))
            link(dve.tensor_scalar(halfs[:, 1, :], halfs[:, 1, :], 0.5, None, ALU.mult))
            mix(0, 0)
            group2(0, 0)
            group2(1, 1)
            LINKS = 6
            with dve.Fori(1, BATCH - 1) as n:
                link.before(n - 1, LINKS)
                group2(2 * n, 0)
                group2(2 * n + 1, 1, pieces=[n - 1])
            link.after(BATCH - 2, LINKS)
            group2(GROUPS - 2, 0)
            group2(GROUPS - 1, 1, ahead=False, pieces=[BATCH - 2, BATCH - 1])
            dve.wait_ge(w4_ready, BATCH)
            dve.tensor_reduce(low_sum[:], low_any[:], AX.X, ALU.max).then_inc(w4_ready, 1)
            dve.wait_ge(low_counted, 1)
            dve.tensor_copy(low_count[:], psum[7][0:1, 0:1]).then_inc(low_known, 1)

            SUMS, Y3 = psum[2:5], psum[6]

            def elu(t, k):
                dve.wait_ge(l_qread, t + 1)
                dve.scalar_tensor_tensor(out=phi[k % 4][:], in0=ex3[k % 2][:], scalar=1.0, in1=relu3[k % 2][:],
                                         op0=ALU.min, op1=ALU.add).then_inc(l_phi, 1)

            def low_kv(t, k):
                dve.wait_ge(l_kvh, t + 1)
                hs = slice(0, SPLIT[1][1])
                dve.tensor_tensor(kvl[k % 2][:, hs], kv[k % 2][:, hs], kvh[k % 2][:, hs].bitcast(F32), ALU.subtract).then_inc(l_kvl, 1)

            def attend(t, k, part):
                lo, hi = SPLIT[part]
                n = hi - lo
                dve.wait_ge(l_cum, 3 * t + part + 1)
                if part == 0:
                    dve.wait_ge(l_phi, t + 1)
                q = phi[k % 4][:, 0, lo * HD:hi * HD].rearrange("p (h d) -> p h d", d=HD)
                dve.tensor_tensor(prod[:, lo:hi], SUMS[part][:, 0:n * NE * HD].rearrange("p (h e d) -> p h e d", e=NE, d=HD),
                                  q.unsqueeze(2).to_broadcast([P, n, NE, HD]), ALU.mult).then_inc(l_read, 1)

            def finish(t, k):
                quotient, residual, i = there(t), there(t - 1), (k - 1) % 2
                if quotient:
                    dve.wait_ge(l_read, 3 * t + 3)
                    dve.tensor_reduce(num[:], prod[:], AX.X, ALU.add).then_inc(l_num, 1)
                if residual:
                    dve.wait_ge(l_y, t)
                    wait(dve, x3_ready, t - 2)
                    dve.tensor_tensor(z3[i][:], Y3[:, 0:P], tile_of(X, t - 1), ALU.add).then_inc(l_yread, 1)
                if quotient:
                    dve.wait_ge(l_num, t + 1)
                    dve.tensor_scalar(den3[:].unsqueeze(2), num[:, :, HD:NE], EPS_LINEAR, None, ALU.add).then_inc(l_den, 1)
                if residual:
                    dve.wait_ge(l_yread, t)
                    dve.bn_stats(st6[:, 0, :], z3[i][:])
                if quotient:
                    dve.wait_ge(l_den, t + 1)
                    dve.reciprocal(rec3[:], den3[:]).then_inc(l_rec, 1)
                if residual:
                    dve.drain()
                    dve.bn_aggr(mvp[i][:, 0, :], st6[:, 0, :]).then_inc(l_stats, 1)
                if quotient:
                    dve.wait_ge(l_rec, t + 1)
                    wait(dve, l_oT, t)
                    dve.tensor_tensor(o3[:].rearrange("p (h d) -> p h d", d=HD), num[:, :, 0:HD],
                                      rec3[:].unsqueeze(2).to_broadcast([P, HEADS, HD]), ALU.mult).then_inc(l_o, 1)

            def batch3(n):
                for k in range(PER_BATCH):
                    t = PER_BATCH * n + k
                    attend(t, k, 0)
                    attend(t, k, 1)
                    attend(t, k, 2)
                    if there(t + 2):
                        elu(t + 2, k + 2)
                    if there(t + 1):
                        low_kv(t + 1, k + 1)
                    finish(t, k)

            dve.wait_ge(x2_ready, GROUPS)
            for i in range(2):
                ins = dve.memset(va3[i][:], 1.0)
            ins.then_inc(l_ones, 1)
            elu(0, 0)
            elu(1, 1)
            low_kv(0, 0)
            batch3(0)
            with dve.Fori(1, BATCH - 1) as n:
                batch3(n)
            batch3(BATCH - 1)
            finish(TILES, 0)

            U4, V4, T4, Y4 = psum[0:2], psum[2:4], psum[6], psum[7]

            def low_x(g):
                dve.wait_ge(g_xTh, g + 1)
                dve.tensor_tensor(xTl[:], T4[:], xTh[:].bitcast(F32), ALU.subtract).then_inc(g_xT, 1)

            def gate(g, o):
                i = o % 2
                dve.wait_ge(g_th, HC * g + o + 1)
                link(dve.scalar_tensor_tensor(out=t4[i][:], in0=th4[i][:], scalar=1.0, in1=U4[i][:],
                                              op0=ALU.add, op1=ALU.mult))
                dve.wait_ge(g_v, HC * g + o + 1)
                wait(dve, g_ha, HC * g + o - 1)
                dve.scalar_tensor_tensor(out=gated[i][:], in0=t4[i][:], scalar=halfs[:, 1, o:o + 1], in1=V4[i][:],
                                         op0=ALU.mult, op1=ALU.mult).then_inc(g_gate, 1)

            def low_hidden(g, o, high, low, done, ready):
                dve.wait_ge(done, HC * g + o + 1)
                dve.tensor_tensor(low[:, o, :], hid[o % 2][:], high[:, o, :].bitcast(F32), ALU.subtract).then_inc(ready, 1)

            def residual4(g):
                dve.wait_ge(g_y, g + 1)
                dve.tensor_tensor(y4[:], Y4[:].rearrange("p (t n) -> p t n", t=GT),
                                  s3[:].unsqueeze(1).to_broadcast([P, GT, P]), ALU.mult).then_inc(g_yread, 1)
                wait(dve, x4_ready, g)
                dve.wait_ge(g_yread, g + 1)
                dve.tensor_tensor(zt[0][:], y4[:], X[:, bass.ds(GT * g, GT), :], ALU.add).then_inc(g_z, 1)
                dve.wait_ge(g_z, g + 1)
                statistics(zt[0][:], mvp[0], GT, g_stats)

            def steps(g):
                ahead = there(g + 1, GROUPS)
                for o in range(HC):
                    low_hidden(g, o, hbh, hbl, g_act1, g_hb)
                    if ahead and o in (1, 2):
                        gate(g + 1, o - 1)
                for o in range(HC):
                    low_hidden(g, o, hch, hcl, g_act2, g_hc)
                    if ahead and o < 2:
                        gate(g + 1, o + 2)
                    if o == 2 and there(g - 1, GROUPS):
                        residual4(g - 1)
                if there(g + 2, GROUPS):
                    low_x(g + 2)

            dve.wait_ge(x3_ready, TILES)
            low_x(0)
            for o in range(HC):
                gate(0, o)
            low_x(1)
            steps(0)
            LINKS = HC
            with dve.Fori(1, GROUPS - 2) as g:
                link.before(g - 1, LINKS)
                steps(g)
            link.after(GROUPS - 3, LINKS)
            steps(GROUPS - 2)
            steps(GROUPS - 1)
            residual4(GROUPS - 1)

        @block.gpsimd
        def _(pool):
            link = Chain(pool, pool_own)
            pool.wait_ge(consts_ready, 2)

            def inverse_std(r, m, count):
                link(pool.tensor_tensor(r[:, 0:count].unsqueeze(2), m[:, 0:count, 1:2], eps[:, 0:count].unsqueeze(2), ALU.add))
                link(pool.tensor_tensor(r[:, 0:count], r[:, 0:count], half[:, 0:count], ALU.pow))

            def spread(col):
                return col.unsqueeze(2).to_broadcast([P, col.shape[1], P])

            def inner_norm(w):
                if isinstance(w, int) and w == 0:
                    pool.wait_ge(x_in, 16 * BATCH)
                pool.wait_ge(y_stats, w + 1)
                inverse_std(rs, mv, 1)
                link(pool.tensor_tensor(z1[:], fused[:], mv[:, 0, 0:1].to_broadcast([P, P]), ALU.subtract))
                link(pool.tensor_tensor(z1[:], z1[:], rs[:, 0:1].to_broadcast([P, P]), ALU.mult))
                link(pool.tensor_tensor(z1[:], z1[:], gamma[:], ALU.mult))
                pool.tensor_tensor(z1[:], z1[:], beta[:], ALU.add)
                pool.drain()
                pool.tensor_tensor(z1[:], z1[:], tile_of(X, w), ALU.add).then_inc(z_ready, 1)

            def outer_norm(w):
                pool.wait_ge(z_stats, w + 1)
                inverse_std(rs2, mv2, 1)
                pool.tensor_tensor(z1[:], z1[:], mv2[:, 0, 0:1].to_broadcast([P, P]), ALU.subtract)
                pool.drain()
                pool.tensor_tensor(tile_of(X, w), z1[:], rs2[:, 0:1].to_broadcast([P, P]), ALU.mult).then_inc(x1_ready, 1)

            def split_values(u, b):
                pool.wait_ge(qkv_read, u + 1)
                one = ones.rearrange("p (h d) -> p h d", d=HD)
                v, part = v32[b][:], [vs[b][:, :, c * HD:(c + 1) * HD] for c in range(VP)]
                wait(pool, o_done, u - 1)
                link(pool.tensor_tensor(part[0], v, one, ALU.mult))
                link(pool.tensor_tensor(vr[:], v, part[0], ALU.subtract))
                link(pool.tensor_tensor(part[1], vr[:], one, ALU.mult))
                pool.tensor_tensor(part[2], vr[:], part[1], ALU.subtract).then_inc(v_ready, 1)
                pool.wait_ge(v_ready, u + 1)

            def low_part(u, b, g):
                pool.wait_ge(high_ready, G * u + g + 1)
                pool.tensor_tensor(prl[:, b, g, :], probs[:, b, g, :], prh[:, b, g, :], ALU.subtract).then_inc(lo_ready[0], 1)

            def steps(w, i):
                for b in range(2):
                    u, r = 2 * w + b, 2 * i + b
                    if there(u, UNITS):
                        low_part(u, b, 0)
                        low_part(u, b, 1)
                    if there(u + 1, UNITS):
                        split_values(u + 1, 1 - b)
                    if there(w - 2):
                        (inner_norm, outer_norm)[b](w - 2)

            LINKS = 2 * (7 + 2 * 3)
            windows(pool, steps, link, LINKS)

            def norm(stats, ready, n, z, m, first_tile, count):
                pool.wait_ge(stats, n + 1)
                inverse_std(rs, m, count)
                pool.tensor_tensor(z, z, spread(m[:, 0:count, 0]), ALU.subtract)
                pool.drain()
                pool.tensor_tensor(X[:, bass.ds(first_tile, count), :], z, spread(rs[:, 0:count]), ALU.mult).then_inc(ready, 1)
                pool.wait_ge(ready, n + 1)

            pool.wait_ge(weights_in, 16 * len(loads))

            def copy(dst, src, row=None):
                one = ones if len(src.shape) == 2 else ones.unsqueeze(1).to_broadcast([P, src.shape[1], P])
                rows = slice(0, P) if row is None else slice(row, row + 1)
                return pool.tensor_tensor(dst[rows], src[rows], one[rows], ALU.mult)

            rest = [fsplit[:, 0], fsplit[:, 1]]
            copy(upper_r[:], upper)
            link(copy(lower_r[:], lower))
            link(copy(b3, bqkvo, 0))
            link(copy(bsplit[:], bqkvo[:]))
            link(pool.tensor_tensor(rest[0], bqkvo[:], bsplit[:], ALU.subtract))
            link(copy(b3, rest[0], 32))
            link(copy(bsplit[:], rest[0]))
            link(pool.tensor_tensor(rest[1], rest[0], bsplit[:], ALU.subtract))
            link(copy(b3, rest[1], 64))

            with pool.Fori(0, BATCH) as n:
                link.before(n, 4)
                for h in range(2):
                    norm(f_stats, x2_ready, 2 * n + h, zt[h][:], mvp[h], (2 * n + h) * GT, GT)
            link.after(BATCH, 4)

            def products(t, k):
                pool.wait_ge(l_phi, t + 1)
                wait(pool, l_kvl, t - 1)
                wait(pool, l_kvl2, t - 1)
                pool.tensor_tensor(kv[k % 2][:], va3[k % 2][:].unsqueeze(3).to_broadcast([P, HEADS, NE, HD]),
                                   phi[k % 4][:, 1, :].rearrange("p (h d) -> p h d", d=HD).unsqueeze(2)
                                   .to_broadcast([P, HEADS, NE, HD]), ALU.mult).then_inc(l_kv, 1)

            def low_kv(t, k):
                pool.wait_ge(l_kvh, t + 1)
                hs = slice(SPLIT[2][0], HEADS)
                pool.tensor_tensor(kvl[k % 2][:, hs], kv[k % 2][:, hs], kvh[k % 2][:, hs].bitcast(F32), ALU.subtract).then_inc(l_kvl2, 1)

            def batch3(n):
                for k in range(PER_BATCH):
                    t = PER_BATCH * n + k
                    if there(t + 1):
                        low_kv(t + 1, k + 1)
                    if there(t + 2):
                        products(t + 2, k + 2)
                    if there(t - 1):
                        i = (k - 1) % 2
                        norm(l_stats, x3_ready, t - 1, z3[i][:].unsqueeze(1), mvp[i], t - 1, 1)

            products(0, 0)
            products(1, 1)
            low_kv(0, 0)
            batch3(0)
            LINKS = 2 * PER_BATCH
            with pool.Fori(1, BATCH - 1) as n:
                link.before(n - 1, LINKS)
                batch3(n)
            link.after(BATCH - 2, LINKS)
            batch3(BATCH - 1)
            norm(l_stats, x3_ready, TILES - 1, z3[1][:].unsqueeze(1), mvp[1], TILES - 1, 1)

            def low_gated(g):
                for o in range(HC):
                    pool.wait_ge(g_hah, HC * g + o + 1)
                    pool.tensor_tensor(hal[:, o, :], gated[o % 2][:], hah[:, o, :].bitcast(F32), ALU.subtract).then_inc(g_ha, 1)

            def steps(g):
                if there(g + 1, GROUPS):
                    low_gated(g + 1)
                if there(g - 1, GROUPS):
                    norm(g_stats, x4_ready, g - 1, zt[0][:], mvp[0], GT * (g - 1), GT)

            low_gated(0)
            steps(0)
            LINKS = 2
            with pool.Fori(1, GROUPS - 1) as g:
                link.before(g - 1, LINKS)
                steps(g)
            link.after(GROUPS - 2, LINKS)
            steps(GROUPS - 1)
            steps(GROUPS)


def kernel(**inputs):
    from concourse import bacc
    from concourse.bass_utils import run_bass_kernel_spmd

    v = {n: np.asarray(x) for n, x in inputs.items()}
    L0, F0, L1, F1 = "L0_attn_", "L0_ffn_", "L1_attn_", "L1_ffn_"
    x = v[L0 + "x"].reshape(BATCH * SEQ, P)
    arrays = {
        "x": x, "xT": x.T, "cst": constants(),
        "projT0": v[L0 + "proj_local"].T, "projT1": v[L0 + "proj_global"].T,
        "fusion": v[L0 + "fusion_w"], "gamma": v[L0 + "ln_gamma"], "beta": v[L0 + "ln_beta"],
        "wrT": v[F0 + "W_r"].T, "wkT": v[F0 + "W_k"].T, "wvT": v[F0 + "W_v"].T,
        "mu": np.stack([v[F0 + "mu_r"], v[F0 + "mu_k"]], axis=1), "w3_s": v[F1 + "w3_s"],
        "scol": np.stack([v[F1 + n].reshape(HC, P).T for n in ("w1_s", "w2_s", "h1_s", "h2_s")], axis=1),
        "w1T": v[F1 + "w1_w"].T, "w2T": v[F1 + "w2_w"].T, "w3T": v[F1 + "w3_w"].T,
        "h1T": v[F1 + "h1_w"].T, "h2T": v[F1 + "h2_w"].T,
    }
    for b, n in enumerate("lg"):
        arrays[f"winT{b}"] = v[f"{L0}W{n}_in"].T
        arrays[f"bin{b}"] = v[f"{L0}b{n}_in"]
        arrays[f"bcol{b}"] = v[f"{L0}b{n}_in"].reshape(3, P).T
        arrays[f"woutT{b}"] = v[f"{L0}W{n}_out"].T
        arrays[f"bout{b}"] = v[f"{L0}b{n}_out"]
    for n in "qkvo":
        arrays[f"lw{n}T"] = v[f"{L1}W{n}"].T
        arrays[f"lb{n}"] = v[f"{L1}b{n}"]
    arrays = {n: np.ascontiguousarray(t) for n, t in arrays.items()}

    nc = bacc.Bacc("TRN2", target_bir_lowering=False, num_devices=1)
    dram = {n: nc.dram_tensor(f"in_{n}", t.shape, mybir.dt.from_np(t.dtype), kind="ExternalInput").ap()
            for n, t in arrays.items()}
    out = nc.dram_tensor("out_y", [BATCH * SEQ, P], F32, kind="ExternalOutput").ap()
    build(nc, dram, out)
    r = run_bass_kernel_spmd(nc, [{f"in_{n}": t for n, t in arrays.items()}], core_ids=[0])
    return r.results[0]["out_y"].reshape(BATCH, SEQ, P)
```
